# Optimizing a Trainium2 kernel written in Bass

```python
import numpy as np
import jax
import jax.numpy as jnp

def _softmax(x, axis=-1):
    return jax.nn.softmax(x, axis=axis)

def _gelu(x):
    return jax.nn.gelu(x, approximate=True)

def _silu(x):
    return jax.nn.silu(x)

def _sigmoid(x):
    return jax.nn.sigmoid(x)

def _layernorm(x, axis=-1, eps=1e-05):
    m = jnp.mean(x, axis=axis, keepdims=True)
    v = jnp.var(x, axis=axis, keepdims=True)
    return (x - m) / jnp.sqrt(v + eps)

def _scatter_add(tgt, idx, src, axis=0):
    return tgt.at[idx].add(src)

def _segment_sum(src, seg, n):
    return jax.ops.segment_sum(src, seg, n)
kernel_name = 'mk_flamingo_gated_d1_seqx_r4_d407d1'

def setup_inputs(seed: int=0):
    np.random.seed(seed)
    _w = jnp.asarray

    def _rec_inputs():
        import jax
        import jax.numpy as jnp
        _rk = jax.random.key(seed)
        x = 4.136e-05 + 0.9999 * jax.random.normal(jax.random.fold_in(_rk, 1), (4, 512, 512), jnp.float32)
        _lenS = 512 - jax.random.randint(jax.random.fold_in(_rk, 7), (4,), 0, max(1, 512 // 4) + 1, jnp.int32)
        _lenS2 = 512 - jax.random.randint(jax.random.fold_in(_rk, 8), (4,), 0, max(1, 512 // 4) + 1, jnp.int32)
        _ctx_1024P = jax.random.normal(jax.random.fold_in(_rk, 11), (4, 16, 256), jnp.float32)
        _ctx_1024c = jax.random.dirichlet(jax.random.fold_in(_rk, 511), 0.3 * jnp.ones((16,), jnp.float32), (4, 512))
        _ctx_1024t = jnp.einsum('bsk,bkd->bsd', _ctx_1024c, _ctx_1024P)
        _ctx_1024t = _ctx_1024t * jax.lax.rsqrt(jnp.mean(jnp.square(_ctx_1024t)) + 1e-12) * 0.953939
        ctx_1024 = -0.000292821 + 1.00034 * (_ctx_1024t + 0.3 * jax.random.normal(jax.random.fold_in(_rk, 611), (4, 512, 256), jnp.float32))
        _g = jax.random.normal(jax.random.fold_in(_rk, 9001), (2, 1), jnp.float32)
        _g = jnp.sign(_g) * jnp.maximum(jnp.abs(_g), 1.0) + (_g == 0) * 1.0
        g_xattn = _g[0]
        g_ffn = _g[1]
        return (x, ctx_1024, g_xattn, g_ffn)
    x, ctx_1024, g_xattn, g_ffn = _rec_inputs()

    def _L0_xattn_setup():
        import jax, jax.numpy as jnp
        import numpy as np
        import math
        B, L, DM = (2, 512, 256)
        DS, DC, EXP = (16, 4, 2)
        DI = EXP * DM
        DR = math.ceil(DM / 16)
        DT_MIN, DT_MAX, DT_FLOOR = (0.001, 0.1, 0.0001)

        def _ssm_forward(hidden_states, z, in_proj_w, conv_w, conv_b, x_proj_w, dt_proj_w, dt_proj_b, A_log, D):
            b = hidden_states.shape[0]
            x = jnp.einsum('ed,bld->bel', in_proj_w, hidden_states)
            xp = jnp.pad(x, ((0, 0), (0, 0), (DC - 1, 0)))
            xc = jax.lax.conv_general_dilated(xp, conv_w[:, None, :], window_strides=(1,), padding='VALID', dimension_numbers=('NCH', 'OIH', 'NCH'), feature_group_count=DI)
            u = jax.nn.silu(xc + conv_b[None, :, None])
            x_dbl = jnp.einsum('ke,bel->bkl', x_proj_w, u)
            dt_lo = x_dbl[:, :DR]
            Bm = x_dbl[:, DR:DR + DS]
            Cm = x_dbl[:, DR + DS:]
            delta = jax.nn.softplus(jnp.einsum('er,brl->bel', dt_proj_w, dt_lo) + dt_proj_b[None, :, None])
            A = -jnp.exp(A_log)

            def step(state, xs):
                d_t, B_t, C_t, u_t = xs
                dA = jnp.exp(d_t[..., None] * A)
                state = state * dA + (d_t * u_t)[..., None] * B_t[:, None, :]
                y_t = jnp.einsum('ben,bn->be', state, C_t)
                return (state, y_t)
            xs = (jnp.moveaxis(delta, -1, 0), jnp.moveaxis(Bm, -1, 0), jnp.moveaxis(Cm, -1, 0), jnp.moveaxis(u, -1, 0))
            state0 = jnp.zeros((b, DI, DS), delta.dtype)
            _, ys = jax.lax.scan(step, state0, xs)
            y = jnp.moveaxis(ys, 0, -1)
            y = y + D[None, :, None] * u
            y = y * jax.nn.silu(z)
            return jnp.swapaxes(y, 1, 2)
        key = jax.random.key(seed)
        ks = jax.random.split(key, 8)
        hidden_states = jax.random.normal(ks[0], (B, L, DM), jnp.float32)
        z = jax.random.normal(ks[1], (B, DI, L), jnp.float32)
        in_proj_w = jax.random.normal(ks[2], (DI, DM), jnp.float32) * DM ** (-0.5)
        conv_w = jax.random.normal(ks[3], (DI, DC), jnp.float32) * DC ** (-0.5)
        conv_b = jnp.zeros((DI,), jnp.float32)
        x_proj_w = jax.random.normal(ks[4], (DR + 2 * DS, DI), jnp.float32) * DI ** (-0.5)
        dt_std = DR ** (-0.5)
        dt_proj_w = jax.random.uniform(ks[5], (DI, DR), jnp.float32, -dt_std, dt_std)
        dt = jnp.exp(jax.random.uniform(ks[6], (DI,), jnp.float32) * (math.log(DT_MAX) - math.log(DT_MIN)) + math.log(DT_MIN))
        dt = jnp.clip(dt, DT_FLOOR)
        dt_proj_b = dt + jnp.log(-jnp.expm1(-dt))
        A_log = jnp.log(jnp.broadcast_to(jnp.arange(1, DS + 1, dtype=jnp.float32), (DI, DS)))
        D = jnp.ones((DI,), jnp.float32)
        return dict(hidden_states=hidden_states, z=z, in_proj_w=in_proj_w, conv_w=conv_w, conv_b=conv_b, x_proj_w=x_proj_w, dt_proj_w=dt_proj_w, dt_proj_b=dt_proj_b, A_log=A_log, D=D)
    _L0_xattn_all = _L0_xattn_setup()
    _L0_xattn_in = {k: v for k, v in _L0_xattn_all.items() if k in ('in_proj_w', 'conv_w', 'conv_b', 'x_proj_w', 'dt_proj_w', 'dt_proj_b', 'A_log', 'D')}
    del _L0_xattn_all

    def _L0_ffn_setup():
        import jax, jax.numpy as jnp
        import numpy as np
        E = 8
        TOP_K = 2
        H = 512
        I_MOE = 352
        I_SH = 1408
        B, S = (2, 512)

        def _moe_forward(hidden_states, router_weight, gate_up_proj, down_proj, sh_gate_w, sh_up_w, sh_down_w, shared_gate_w):
            b, s, h = hidden_states.shape
            x = hidden_states.reshape(-1, h)
            shared = jnp.einsum('ti,hi->th', jax.nn.silu(x @ sh_gate_w.T) * (x @ sh_up_w.T), sh_down_w)
            logits = x @ router_weight.T
            probs = jax.nn.softmax(logits.astype(jnp.float32), axis=-1)
            top_v, top_i = jax.lax.top_k(probs, TOP_K)
            top_v = top_v / top_v.sum(axis=-1, keepdims=True)
            combine = (jax.nn.one_hot(top_i, E, dtype=top_v.dtype) * top_v[..., None]).sum(axis=1)
            out = jnp.zeros_like(x)
            for e in range(E):
                gu = x @ gate_up_proj[e].T
                gate, up = (gu[:, :I_MOE], gu[:, I_MOE:])
                cur = jax.nn.silu(gate) * up @ down_proj[e].T
                out = out + cur * combine[:, e:e + 1]
            out = out + jax.nn.sigmoid(x @ shared_gate_w.T) * shared
            return out.reshape(b, s, h)
        key = jax.random.key(seed)
        ks = jax.random.split(key, 8)
        scale = 0.02
        return {'hidden_states': jax.random.normal(ks[0], (B, S, H), dtype=jnp.float32), 'router_weight': jax.random.normal(ks[1], (E, H), dtype=jnp.float32) * scale, 'gate_up_proj': jax.random.normal(ks[2], (E, 2 * I_MOE, H), dtype=jnp.float32) * scale, 'down_proj': jax.random.normal(ks[3], (E, H, I_MOE), dtype=jnp.float32) * scale, 'sh_gate_w': jax.random.normal(ks[4], (I_SH, H), dtype=jnp.float32) * scale, 'sh_up_w': jax.random.normal(ks[5], (I_SH, H), dtype=jnp.float32) * scale, 'sh_down_w': jax.random.normal(ks[6], (H, I_SH), dtype=jnp.float32) * scale, 'shared_gate_w': jax.random.normal(ks[7], (1, H), dtype=jnp.float32) * scale}
    _L0_ffn_all = _L0_ffn_setup()
    _L0_ffn_in = {k: v for k, v in _L0_ffn_all.items() if k in ('router_weight', 'gate_up_proj', 'down_proj', 'sh_gate_w', 'sh_up_w', 'sh_down_w', 'shared_gate_w')}
    del _L0_ffn_all
    return {'x': x, 'ctx_1024': ctx_1024, 'g_xattn': g_xattn, 'g_ffn': g_ffn, 'L0_xattn_in_proj_w': _L0_xattn_in['in_proj_w'], 'L0_xattn_conv_w': _L0_xattn_in['conv_w'], 'L0_xattn_conv_b': _L0_xattn_in['conv_b'], 'L0_xattn_x_proj_w': _L0_xattn_in['x_proj_w'], 'L0_xattn_dt_proj_w': _L0_xattn_in['dt_proj_w'], 'L0_xattn_dt_proj_b': _L0_xattn_in['dt_proj_b'], 'L0_xattn_A_log': _L0_xattn_in['A_log'], 'L0_xattn_D': _L0_xattn_in['D'], 'L0_ffn_router_weight': _L0_ffn_in['router_weight'], 'L0_ffn_gate_up_proj': _L0_ffn_in['gate_up_proj'], 'L0_ffn_down_proj': _L0_ffn_in['down_proj'], 'L0_ffn_sh_gate_w': _L0_ffn_in['sh_gate_w'], 'L0_ffn_sh_up_w': _L0_ffn_in['sh_up_w'], 'L0_ffn_sh_down_w': _L0_ffn_in['sh_down_w'], 'L0_ffn_shared_gate_w': _L0_ffn_in['shared_gate_w']}

def reference(x, ctx_1024, g_xattn, g_ffn, L0_xattn_in_proj_w, L0_xattn_conv_w, L0_xattn_conv_b, L0_xattn_x_proj_w, L0_xattn_dt_proj_w, L0_xattn_dt_proj_b, L0_xattn_A_log, L0_xattn_D, L0_ffn_router_weight, L0_ffn_gate_up_proj, L0_ffn_down_proj, L0_ffn_sh_gate_w, L0_ffn_sh_up_w, L0_ffn_sh_down_w, L0_ffn_shared_gate_w):
    import jax
    import jax.numpy as jnp

    def _L0_xattn_ref(hidden_states, z, in_proj_w, conv_w, conv_b, x_proj_w, dt_proj_w, dt_proj_b, A_log, D):
        import jax, jax.numpy as jnp
        import numpy as np
        import math
        B, L, DM = (2, 512, 256)
        DS, DC, EXP = (16, 4, 2)
        DI = EXP * DM
        DR = math.ceil(DM / 16)
        DT_MIN, DT_MAX, DT_FLOOR = (0.001, 0.1, 0.0001)

        def _ssm_forward(hidden_states, z, in_proj_w, conv_w, conv_b, x_proj_w, dt_proj_w, dt_proj_b, A_log, D):
            b = hidden_states.shape[0]
            x = jnp.einsum('ed,bld->bel', in_proj_w, hidden_states)
            xp = jnp.pad(x, ((0, 0), (0, 0), (DC - 1, 0)))
            xc = jax.lax.conv_general_dilated(xp, conv_w[:, None, :], window_strides=(1,), padding='VALID', dimension_numbers=('NCH', 'OIH', 'NCH'), feature_group_count=DI)
            u = jax.nn.silu(xc + conv_b[None, :, None])
            x_dbl = jnp.einsum('ke,bel->bkl', x_proj_w, u)
            dt_lo = x_dbl[:, :DR]
            Bm = x_dbl[:, DR:DR + DS]
            Cm = x_dbl[:, DR + DS:]
            delta = jax.nn.softplus(jnp.einsum('er,brl->bel', dt_proj_w, dt_lo) + dt_proj_b[None, :, None])
            A = -jnp.exp(A_log)

            def step(state, xs):
                d_t, B_t, C_t, u_t = xs
                dA = jnp.exp(d_t[..., None] * A)
                state = state * dA + (d_t * u_t)[..., None] * B_t[:, None, :]
                y_t = jnp.einsum('ben,bn->be', state, C_t)
                return (state, y_t)
            xs = (jnp.moveaxis(delta, -1, 0), jnp.moveaxis(Bm, -1, 0), jnp.moveaxis(Cm, -1, 0), jnp.moveaxis(u, -1, 0))
            state0 = jnp.zeros((b, DI, DS), delta.dtype)
            _, ys = jax.lax.scan(step, state0, xs)
            y = jnp.moveaxis(ys, 0, -1)
            y = y + D[None, :, None] * u
            y = y * jax.nn.silu(z)
            return jnp.swapaxes(y, 1, 2)
        return _ssm_forward(hidden_states, z, in_proj_w, conv_w, conv_b, x_proj_w, dt_proj_w, dt_proj_b, A_log, D)

    def _L0_ffn_ref(hidden_states, router_weight, gate_up_proj, down_proj, sh_gate_w, sh_up_w, sh_down_w, shared_gate_w):
        import jax, jax.numpy as jnp
        import numpy as np
        E = 8
        TOP_K = 2
        H = 512
        I_MOE = 352
        I_SH = 1408
        B, S = (2, 512)

        def _moe_forward(hidden_states, router_weight, gate_up_proj, down_proj, sh_gate_w, sh_up_w, sh_down_w, shared_gate_w):
            b, s, h = hidden_states.shape
            x = hidden_states.reshape(-1, h)
            shared = jnp.einsum('ti,hi->th', jax.nn.silu(x @ sh_gate_w.T) * (x @ sh_up_w.T), sh_down_w)
            logits = x @ router_weight.T
            probs = jax.nn.softmax(logits.astype(jnp.float32), axis=-1)
            top_v, top_i = jax.lax.top_k(probs, TOP_K)
            top_v = top_v / top_v.sum(axis=-1, keepdims=True)
            combine = (jax.nn.one_hot(top_i, E, dtype=top_v.dtype) * top_v[..., None]).sum(axis=1)
            out = jnp.zeros_like(x)
            for e in range(E):
                gu = x @ gate_up_proj[e].T
                gate, up = (gu[:, :I_MOE], gu[:, I_MOE:])
                cur = jax.nn.silu(gate) * up @ down_proj[e].T
                out = out + cur * combine[:, e:e + 1]
            out = out + jax.nn.sigmoid(x @ shared_gate_w.T) * shared
            return out.reshape(b, s, h)
        return _moe_forward(hidden_states, router_weight, gate_up_proj, down_proj, sh_gate_w, sh_up_w, sh_down_w, shared_gate_w)
    x = x + jnp.tanh(g_xattn[0]) * _L0_xattn_ref(ctx_1024, _layernorm(x, axis=-1), L0_xattn_in_proj_w, L0_xattn_conv_w, L0_xattn_conv_b, L0_xattn_x_proj_w, L0_xattn_dt_proj_w, L0_xattn_dt_proj_b, L0_xattn_A_log, L0_xattn_D)
    x = x + jnp.tanh(g_ffn[0]) * _L0_ffn_ref(_layernorm(x, axis=-1), L0_ffn_router_weight, L0_ffn_gate_up_proj, L0_ffn_down_proj, L0_ffn_sh_gate_w, L0_ffn_sh_up_w, L0_ffn_sh_down_w, L0_ffn_shared_gate_w)
    return x

_drawn_inputs = setup_inputs


def setup_inputs(seed=0):
    import zlib

    import numpy as np

    out = dict(_drawn_inputs(seed))
    spreads = {'L0_xattn_conv_b': (0.0, 0.277), 'L0_xattn_D': (1.0, 0.2)}
    factors = {'L0_xattn_dt_proj_w': 6.598, 'L0_xattn_dt_proj_b': 2.912, 'L0_ffn_shared_gate_w': 7.205}
    for name, (base, spread) in spreads.items():
        noise = np.random.default_rng([zlib.crc32(name.encode()), seed]).standard_normal(out[name].shape)
        drawn = base * np.exp(spread * noise) if base else spread * noise
        out[name] = jnp.asarray(drawn.astype(out[name].dtype))
    for name, factor in factors.items():
        out[name] = (out[name] * factor).astype(out[name].dtype)
    return out
```

```python
from contextlib import ExitStack

import numpy as np

import concourse.bass as bass
from concourse import mybir

ALU = mybir.AluOpType
ACT = mybir.ActivationFunctionType
F32 = mybir.dt.float32
F16 = mybir.dt.float16
U32 = mybir.dt.uint32

P = 128
B, L, DI = 4, 512, 512
DM = 256
DS, DC = 16, 4
DR = 16
E, I_MOE, I_SH = 8, 352, 1408
ET = DI // P
KT = DM // P
XD = DR + 2 * DS
NP = DS // 2
SL = NP * ET
CH = (E * I_MOE + I_SH) // P
SH_ROWS = I_SH // I_MOE
TROWS = E + SH_ROWS
R = E + 1
HALF = 3 * 512
EPS = 1e-5
WS = 64.0
HS = 8.0
SEED = 2
LOOPS = CH // ET


def chunk_segments(c):
    out, p = [], 0
    while p < P:
        row = (c * P + p) // I_MOE
        q = min(P, (row + 1) * I_MOE - c * P)
        out.append((p, q, row))
        p = q
    return out


def program(nc, x_nat, x_t, ctx_t, g_xattn, g_ffn, win_t, conv_w, conv_b, xproj_t, dt_t, dt_b, a_log, d_skip,
            router_t, w_raw, ident_in, out):
    w_split = nc.dram_tensor("w_split", [CH, P, 2 * HALF], F16, kind="Internal").ap()
    bc_dram = nc.dram_tensor("bc_dram", [2 * DS, L], F32, kind="Internal").ap()
    table_dram = nc.dram_tensor("table_dram", [TROWS, L], F32, kind="Internal").ap()

    with ExitStack() as ctx:
        def sb(name, shape, dt=F32):
            return ctx.enter_context(nc.sbuf_tensor(name, shape, dt))

        def psum(name, shape):
            return ctx.enter_context(nc.psum_tensor(name, shape, F32))

        def sem(name):
            return ctx.enter_context(nc.semaphore(name))

        win = sb("win", [P, KT, DI])
        cw = sb("cw", [P, ET, DC])
        cbias = sb("cbias", [P, ET])
        xproj = sb("xproj", [P, ET, XD])
        dtw = sb("dtw", [DR, DI])
        dtb = sb("dtb", [P, ET])
        amat = sb("amat", [P, ET, DS])
        dhalf = sb("dhalf", [P, ET])
        rout = sb("rout", [P, ET, R])
        ident = sb("ident", [P, P])
        mean_w = sb("mean_w", [P, P])
        zeros16 = sb("zeros16", [P, P], F16)
        gates = sb("gates", [P, 2])
        eps = sb("eps", [P, 1])
        one = sb("one", [P, 1])
        iota = sb("iota", [P, E])
        seedbox = sb("seedbox", [P, 16])
        ctxb = sb("ctxb", [P, KT, L])
        xn = sb("xn", [P, ET, L])
        xt = sb("xt", [P, ET, L])
        x1 = sb("x1", [P, ET, L])
        xh = sb("xh", [P, ET, L], F16)
        xl = sb("xl", [P, ET, L], F16)
        tmp_a = sb("tmp_a", [P, ET, L])
        tmp_b = sb("tmp_b", [P, ET, 516])
        tmp_c = sb("tmp_c", [P, ET, L])
        tb = tmp_b[:, :, 0:L]
        du = sb("du", [P, ET, L])
        delta = sb("delta", [P, ET, L])
        y2 = sb("y2", [P, ET, 2, L])
        xdbl = sb("xdbl", [XD, L])
        stats = sb("stats", [P, ET, 6])
        mv = sb("mv", [P, ET, 2])
        lnv = sb("lnv", [P, ET])
        rstd = sb("rstd", [P, ET])
        lg = sb("lg", [P, ET, 16])
        top = sb("top", [P, ET, 8])
        topi = sb("topi", [P, ET, 8], U32)
        topf = sb("topf", [P, ET, 2])
        gap = sb("gap", [P, ET])
        e2 = sb("e2", [P, ET])
        den = sb("den", [P, ET])
        p1 = sb("p1", [P, ET])
        p2 = sb("p2", [P, ET])
        sg = sb("sg", [P, ET])
        hot = sb("hot", [P, ET, E])
        hot2 = sb("hot2", [P, ET, E])
        comb = sb("comb", [P, ET, TROWS])
        combt = sb("combt", [TROWS, L])
        bc = sb("bc", [P, 2, 4, L])
        da = sb("da", [P, 2, 2, L])
        dbu = sb("dbu", [P, 2, 2, L])
        st = sb("st", [P, 2, 2, L])
        prod = sb("prod", [P, 2, 2, L])
        wring = sb("wring", [P, 4, 2 * HALF], F16)
        scale = sb("scale", [P, 4, L])
        mbuf = sb("mbuf", [P, 6, L])
        w32 = mbuf[:, :, :].rearrange("p (s a) l -> p s (a l)", s=2)
        th, act_a, act_b = mbuf[:, 0, :], mbuf[:, 1, :], mbuf[:, 2, :]
        hf = mbuf[:, 3:6, :]
        hhi = sb("hhi", [P, 3, L], F16)
        hlo = sb("hlo", [P, 3, L], F16)

        acc = psum("acc", [P, ET, L])
        ps_g = psum("ps_g", [P, L])
        ps_u = psum("ps_u", [P, L])
        ps = [psum("ps_0", [P, L]), psum("ps_1", [P, L])]

        names = """consts seeds const_dve const_act const_dve2
            ctx_in xn_in xt_in bn_stats bn_aggr ln1 rstd_ok z_ok tz_ok gate_ok inproj xp_ok pads conv tanh_u u_ok
            xproj_ok xdbl_ok bc_stored dt_ok dtv_ok abs_ok e1_ok ln_ok relu_ok back_ok corr_ok sum1_ok delta_ok y_init
            front_ok bc_in da_ready dbu_ready scan_done prod_ready yadd_done
            ysum yg x1_ok mean_ok xc_ok sq_ok var_ok ln2 rs_ok xnorm xh_ok xl_ok logits lg_ok top_ok topi_ok topf_ok
            gap_ok e2_ok den_ok p1_ok p2_ok hot_ok comb_ok tsg sg_ok combt_ps combt_ok table_ok
            g_ready u_ready g_used u_used tanh_done hmul_done hi_done hlo_done down_done open_ok fin_ok out_done
            prep_hi prep_lo""".split()
        s = {n: sem(n) for n in names}
        raw_in = [sem(f"raw_in{i}") for i in range(2)]
        stored = [sem(f"stored{i}") for i in range(4)]
        w_in = [sem(f"w_in{i}") for i in range(4)]
        scale_in = [sem(f"scale_in{i}") for i in range(4)]

        fills = [len(range(i, CH, 4)) for i in range(4)]
        N_CONST = 14

        block = ctx.enter_context(nc.Block())

        @block.sync
        def _(sp):
            def load_row(bb, first):
                if not first:
                    sp.wait_ge(s["inproj"], ET * bb)
                    sp.wait_ge(s["ysum"], bb)
                    sp.wait_ge(s["yg"], bb)
                sp.dma_start(ctxb[:], ctx_t[bass.ds(bb, 1)].rearrange("b p k l -> p (b k) l")).then_inc(s["ctx_in"], 16)
                sp.dma_start(xn[:], x_nat[bass.ds(bb, 1)].rearrange("b p k l -> p (b k) l")).then_inc(s["xn_in"], 16)

            def load_xt(bb, first):
                if not first:
                    sp.wait_ge(s["x1_ok"], bb)
                sp.dma_start(xt[:], x_t[bass.ds(bb, 1)].rearrange("b p k l -> p (b k) l")).then_inc(s["xt_in"], 16)

            def store_bc(bb):
                sp.wait_ge(s["xdbl_ok"], bb + 1)
                sp.dma_start(bc_dram, xdbl[DR:XD, :]).then_inc(s["bc_stored"], 16)
                sp.wait_ge(s["bc_stored"], 16 * (bb + 1))

            def load_bc(bb, j, peeled_first=False):
                if not peeled_first:
                    sp.wait_ge(s["bc_in"], 16 * (NP * bb + j))
                src = bass.AP(bc_dram.tensor, 2 * L * j, [[0, P], [DS * L, 2], [1, 2 * L]])
                sp.dma_start(bc[:, bass.ds(j % 2, 1), :, :].rearrange("p o (a n) l -> p (o a) (n l)", a=2), src)\
                    .then_inc(s["bc_in"], 16)

            def bc_slot_free(bb, j):
                sp.wait_ge(s["prod_ready"], SL * bb + ET * (j - 1))
                sp.wait_ge(s["dbu_ready"], SL * bb + ET * (j - 1))

            def load_raw(c, slot):
                sp.dma_start(w32[:, slot, :], w_raw[bass.ds(c, 1)].rearrange("c p n -> p (c n)")).then_inc(raw_in[slot], 16)

            def store_split(c, slot):
                sp.dma_start(w_split[bass.ds(c, 1)].rearrange("c p n -> p (c n)"), wring[:, slot, :])\
                    .then_inc(stored[slot], 16)

            def load_w(c, slot):
                sp.dma_start(wring[:, slot, :], w_split[bass.ds(c, 1)].rearrange("c p n -> p (c n)"))\
                    .then_inc(w_in[slot], 16)

            def load_scale(b, c, i, k, j):
                pass

            for n, (dst, src) in enumerate([
                (win[:], win_t), (cw[:], conv_w), (cbias[:], conv_b), (xproj[:], xproj_t), (dtw[:], dt_t),
                (dtb[:], dt_b), (amat[:], a_log), (dhalf[:], d_skip), (rout[:], router_t), (ident[:], ident_in),
                (gates[:, 0:1], bass.AP(g_xattn.tensor, 0, [[0, P], [1, 1]])),
                (gates[:, 1:2], bass.AP(g_ffn.tensor, 0, [[0, P], [1, 1]])),
            ]):
                sp.dma_start(dst, src).then_inc(s["consts"], 16)
            load_row(0, True)
            load_xt(0, True)
            load_raw(0, 0)
            load_raw(1, 1)
            store_bc(0)
            load_bc(0, 0, True)
            load_bc(0, 1)

            def prep_trip(j, last):
                for i in range(4):
                    c = 4 * j + i
                    sp.wait_ge(s["prep_lo"], c + 1)
                    store_split(c, i)
                    if not (last and i == 3):
                        load_raw(c + 2, i % 2)
                if not last:
                    bc_slot_free(0, j + 2)
                    load_bc(0, j + 2)
            with sp.Fori(0, LOOPS - 2) as j:
                prep_trip(j, False)
            for i in range(4):
                c = 4 * (LOOPS - 2) + i
                sp.wait_ge(s["prep_lo"], c + 1)
                store_split(c, i)
                load_raw(c + 2, i % 2)
            prep_trip(LOOPS - 1, True)
            sp.wait_ge(s["prep_lo"], CH)
            store_split(CH - 1, 0)
            for i in range(4):
                sp.wait_ge(stored[i], 16 * fills[i])

            def scale_dmas(b, c):
                for p, q, row in chunk_segments(c):
                    src = bass.AP(table_dram.tensor, L * row, [[0, q - p], [1, L]])
                    sp.dma_start(scale[p:q, c % 4, :], src).then_inc(scale_in[c % 4], 16)

            def mixture_dmas(b, scan_next):
                for i in (1, 2, 3, 0):
                    sp.wait_ge(s["down_done"], SEED + CH * b)
                    load_w(i, i)
                if scan_next:
                    load_row(b + 1, False)
                    load_xt(b + 1, False)
                sp.wait_ge(s["combt_ok"], b + 1)
                sp.dma_start(table_dram, combt[:, :]).then_inc(s["table_ok"], 16)
                sp.wait_ge(s["table_ok"], 16 * (b + 1))
                for c in range(CH):
                    if c >= 4:
                        sp.wait_ge(s["hmul_done"], CH * b + c - 3)
                    scale_dmas(b, c)
                    if scan_next and c == 0:
                        store_bc(b + 1)
                        load_bc(b + 1, 0, True)
                        load_bc(b + 1, 1)
                    if scan_next and c >= 4 and c % 4 == 3 and c // 4 + 1 < NP:
                        bc_slot_free(b + 1, c // 4 + 1)
                        load_bc(b + 1, c // 4 + 1)
                    if c + 4 < CH:
                        sp.wait_ge(s["down_done"], SEED + CH * b + c + 1)
                        load_w(c + 4, c % 4)

            def store_out(b):
                sp.wait_ge(s["fin_ok"], b + 2)
                sp.dma_start(out[bass.ds(b, 1)].rearrange("b p k l -> p (b k) l"), tmp_a[:]).then_inc(s["out_done"], 16)

            with sp.Fori(0, B - 1) as b:
                mixture_dmas(b, True)
                store_out(b)
            mixture_dmas(B - 1, False)
            store_out(B - 1)
            sp.wait_ge(s["out_done"], 16 * B)

        @block.tensor
        def _(pe):
            def front(bb, first):
                if not first:
                    pe.wait_ge(s["combt_ok"], bb)
                pe.wait_ge(s["ctx_in"], 16 * (bb + 1))
                for e in range(ET):
                    if e >= 2:
                        pe.wait_ge(s["xp_ok"], ET * bb + e - 1)
                    for k in range(KT):
                        last = pe.matmul(ps[e % 2][:], win[:, k, e * P:(e + 1) * P], ctxb[:, k, :],
                                         start=(k == 0), stop=(k == KT - 1))
                    last.then_inc(s["inproj"], 1)
                pe.wait_ge(s["xp_ok"], ET * bb + ET)
                for e in range(ET):
                    pe.wait_ge(s["u_ok"], ET * bb + e + 1)
                    last = pe.matmul(ps[0][0:XD, :], xproj[:, e, :], du[:, e, :], start=(e == 0), stop=(e == ET - 1))
                last.then_inc(s["xproj_ok"], 1)
                pe.wait_ge(s["xdbl_ok"], bb + 1)
                for e in range(ET):
                    if e >= 2:
                        pe.wait_ge(s["dtv_ok"], ET * bb + e - 1)
                    pe.matmul(ps[e % 2][:], dtw[:, e * P:(e + 1) * P], xdbl[0:DR, :], start=True, stop=True)\
                        .then_inc(s["dt_ok"], 1)

            def link(bb):
                pe.wait_ge(s["dtv_ok"], ET * (bb + 1))
                pe.wait_ge(s["x1_ok"], bb + 1)
                for e in range(ET):
                    last = pe.matmul(ps[0][:], mean_w[:], x1[:, e, :], start=(e == 0), stop=(e == ET - 1))
                last.then_inc(s["mean_ok"], 1)
                pe.wait_ge(s["sq_ok"], bb + 1)
                for e in range(ET):
                    last = pe.matmul(ps[1][:], mean_w[:], tmp_c[:, e, :], start=(e == 0), stop=(e == ET - 1))
                last.then_inc(s["var_ok"], 1)
                pe.wait_ge(s["xnorm"], bb + 1)
                for t in range(ET):
                    for e in range(ET):
                        last = pe.matmul(ps[0][:, t * 16:t * 16 + R], tb[:, e, t * P:(t + 1) * P], rout[:, e, :],
                                         start=(e == 0), stop=(e == ET - 1))
                last.then_inc(s["logits"], 1)
                pe.wait_ge(s["comb_ok"], bb + 1)
                for t in range(ET):
                    last = pe.transpose(ps[1][0:TROWS, t * P:(t + 1) * P], comb[:, t, :], ident[:])
                last.then_inc(s["combt_ps"], 1)

            def wslice(slot, low, part, k):
                at = HALF * low + 512 * part + P * k
                return wring[:, slot, at:at + P]

            def up(b, c_wait, slot, g):
                pe.wait_ge(w_in[slot], c_wait)
                for part, bank, used, ready in ((0, ps_g, "g_used", "g_ready"), (1, ps_u, "u_used", "u_ready")):
                    pe.wait_ge(s[used], g + 1)
                    n = 0
                    for k in range(ET):
                        for low, rhs in ((0, xh), (0, xl), (1, xh)):
                            last = pe.matmul(bank[:], wslice(slot, low, part, k), rhs[:, k, :],
                                             start=(n == 0), stop=(n == 3 * ET - 1))
                            n += 1
                    last.then_inc(s[ready], 1)

            def down(slot, hslot, g, closing=False):
                pe.wait_ge(s["hlo_done"], g + SEED + 1)
                for m in range(ET):
                    for n, (low, rhs) in enumerate(((0, hhi), (0, hlo), (1, hhi))):
                        last = pe.matmul(acc[:, m, :], wslice(slot, low, 2, m), rhs[:, hslot, :],
                                         start=False, stop=(closing and n == 2), skip_group_check=True)
                last.then_inc(s["down_done"], 1)

            def mixture(b):
                pe.wait_ge(s["xl_ok"], b + 1)
                pe.wait_ge(s["fin_ok"], b + 1)
                for m in range(ET):
                    pe.matmul(acc[:, m, :], zeros16[:], xh[:, m, :], start=True, stop=False, skip_group_check=True)
                up(b, 16 * (fills[0] * b + 1), 0, CH * b)
                with pe.Fori(0, LOOPS) as j:
                    for i in range(4):
                        c = 4 * j + i
                        nxt = (i + 1) % 4
                        up(b, 16 * (fills[nxt] * b + j + (2 if i == 3 else 1)), nxt, CH * b + c + 1)
                        down(i, i % 2, CH * b + c)
                down(0, 2, CH * b + CH - 1, closing=True)

            pe.wait_ge(s["consts"], 16 * 12)
            pe.wait_ge(s["const_dve"], 4)
            front(0, True)
            link(0)
            with pe.Fori(0, B - 1) as b:
                front(b + 1, False)
                mixture(b)
                link(b + 1)
            mixture(B - 1)

        @block.scalar
        def _(act):
            def front(bb, first):
                act.wait_ge(s["bn_aggr"], ET * (bb + 1))
                act.activation(lnv[:], mv[:, :, 1], ACT.Ln, bias=eps[:, 0:1]).then_inc(s["ln1"], 1)
                act.wait_ge(s["ln1"], bb + 1)
                act.activation(rstd[:], lnv[:], ACT.Exp, scale=-0.5).then_inc(s["rstd_ok"], 1)
                act.wait_ge(s["pads"], bb + 1)
                for e in range(ET):
                    act.wait_ge(s["inproj"], ET * bb + e + 1)
                    act.activation(tmp_b[:, e, DC - 1:DC - 1 + L], ps[e % 2][:], ACT.Copy).then_inc(s["xp_ok"], 1)
                act.wait_ge(s["z_ok"], ET * (bb + 1))
                act.activation(tmp_a[:], xn[:], ACT.Tanh, scale=0.5).then_inc(s["tz_ok"], 1)
                for e in range(ET):
                    act.wait_ge(s["conv"], DC * (ET * bb + e + 1))
                    act.activation(tmp_c[:, e, :], delta[:, e, :], ACT.Tanh, scale=0.5).then_inc(s["tanh_u"], 1)
                act.wait_ge(s["xproj_ok"], bb + 1)
                act.activation(xdbl[:], ps[0][0:XD, :], ACT.Copy, scale=0.5).then_inc(s["xdbl_ok"], 1)
                for e in range(ET):
                    act.wait_ge(s["dt_ok"], ET * bb + e + 1)
                    act.activation(tb[:, e, :], ps[e % 2][:], ACT.Identity, bias=dtb[:, e:e + 1])\
                        .then_inc(s["dtv_ok"], 1)
                act.wait_ge(s["dtv_ok"], ET * (bb + 1))
                act.wait_ge(s["gate_ok"], bb + 1)
                act.activation(tmp_a[:], tb, ACT.Abs).then_inc(s["abs_ok"], 1)
                act.wait_ge(s["abs_ok"], bb + 1)
                act.activation(tmp_a[:], tmp_a[:], ACT.Exp, scale=-1.0).then_inc(s["e1_ok"], 1)
                act.wait_ge(s["e1_ok"], bb + 1)
                act.activation(tmp_c[:], tmp_a[:], ACT.Ln, bias=one[:, 0:1]).then_inc(s["ln_ok"], 1)

            def decay(gs, j, e):
                act.wait_ge(s["scan_done"], gs + 1)
                act.activation(da[:, e % 2, 0, :], delta[:, e, :], ACT.Exp, scale=amat[:, e, bass.ds(2 * j, 1)])
                act.activation(da[:, e % 2, 1, 1:L], delta[:, e, 1:L], ACT.Exp, scale=amat[:, e, bass.ds(2 * j + 1, 1)])\
                    .then_inc(s["da_ready"], 1)

            def link(bb):
                act.wait_ge(s["xc_ok"], bb + 1)
                act.activation(tmp_c[:], tb, ACT.Square).then_inc(s["sq_ok"], 1)
                act.wait_ge(s["var_ok"], bb + 1)
                act.activation(tmp_a[:, 0, :], ps[1][:], ACT.Ln, bias=eps[:, 0:1]).then_inc(s["ln2"], 1)
                act.wait_ge(s["ln2"], bb + 1)
                act.activation(tmp_a[:, 1, :], tmp_a[:, 0, :], ACT.Exp, scale=-0.5).then_inc(s["rs_ok"], 1)
                act.wait_ge(s["xnorm"], bb + 1)
                act.activation(xh[:], tb, ACT.Copy).then_inc(s["xh_ok"], 1)
                act.wait_ge(s["gap_ok"], bb + 1)
                act.activation(e2[:], gap[:], ACT.Exp).then_inc(s["e2_ok"], 1)
                act.wait_ge(s["lg_ok"], bb + 1)
                act.activation(sg[:], lg[:, :, E], ACT.Tanh, scale=0.5).then_inc(s["tsg"], 1)
                act.wait_ge(s["combt_ps"], bb + 1)
                act.activation(combt[:], ps[1][0:TROWS, :], ACT.Copy).then_inc(s["combt_ok"], 1)

            def squash(g):
                act.wait_ge(s["g_ready"], g + 1)
                act.activation(th, ps_g[:], ACT.Tanh, scale=0.5 / WS).then_inc(s["tanh_done"], 1)

            def high(g, hslot):
                act.wait_ge(s["hmul_done"], g + 1)
                act.wait_ge(s["down_done"], g + 1)
                act.activation(hhi[:, hslot, :], hf[:, hslot, :], ACT.Copy).then_inc(s["hi_done"], 1)

            def split(c, i):
                act.activation(wring[:, i, 0:HALF], w32[:, i % 2, :], ACT.Copy, scale=WS).then_inc(s["prep_hi"], 1)

            act.wait_ge(s["consts"], 16 * 12)
            act.activation(amat[:], amat[:], ACT.Exp).then_inc(s["const_act"], 1)
            act.activation(gates[:], gates[:], ACT.Tanh).then_inc(s["const_act"], 1)
            act.wait_ge(s["const_dve"], 4)
            act.wait_ge(s["const_dve2"], 3)
            front(0, True)
            act.wait_ge(s["front_ok"], 1)
            act.activation(lnv[:], rstd[:], ACT.Exp)
            for i in range(4):
                act.wait_ge(raw_in[i % 2], 16 * (i // 2 + 1))
                decay(i, 0, i)
                split(i, i)
            with act.Fori(1, NP) as j:
                for i in range(4):
                    decay(4 * j + i, j, i)
                    act.wait_ge(raw_in[i % 2], 16 * (2 * j + i // 2 + 1))
                    act.wait_ge(stored[i], 16 * j)
                    split(4 * j + i, i)
            act.wait_ge(raw_in[0], 16 * (CH + 1) // 2)
            act.wait_ge(stored[0], 16 * (fills[0] - 1))
            split(CH - 1, 0)
            link(0)

            def mixture(b, scan_next):
                with act.Fori(0, LOOPS) as j:
                    for i in range(4):
                        g = CH * b + 4 * j + i
                        squash(g)
                        if scan_next:
                            decay(SL * (b + 1) + 4 * j + i, j, i)
                        high(g, i % 2)
                squash(CH * b + CH - 1)
                high(CH * b + CH - 1, 2)

            with act.Fori(0, B - 1) as b:
                front(b + 1, False)
                act.wait_ge(s["front_ok"], b + 2)
                act.activation(lnv[:], rstd[:], ACT.Exp)
                mixture(b, True)
                link(b + 1)
            mixture(B - 1, False)

        @block.vector
        def _(ve):
            def front(bb, first):
                ve.wait_ge(s["xn_in"], 16 * (bb + 1))
                for e in range(ET):
                    ve.bn_stats(stats[:, e, :], xn[:, e, :]).then_inc(s["bn_stats"], 1)
                ve.wait_ge(s["bn_stats"], ET * (bb + 1))
                ve.memset(tmp_b[:, :, 0:DC - 1], 0.0).then_inc(s["pads"], 1)
                for e in range(ET):
                    ve.bn_aggr(mv[:, e, :], stats[:, e, :]).then_inc(s["bn_aggr"], 1)
                ve.wait_ge(s["rstd_ok"], bb + 1)
                for e in range(ET):
                    ve.tensor_scalar(xn[:, e, :], xn[:, e, :], mv[:, e, 0:1], rstd[:, e:e + 1], ALU.subtract, ALU.mult)\
                        .then_inc(s["z_ok"], 1)
                n = DC * ET * bb
                for e in range(ET):
                    ve.wait_ge(s["xp_ok"], ET * bb + e + 1)
                    ve.tensor_scalar(delta[:, e, :], tmp_b[:, e, 0:L], cw[:, e, 0:1], cbias[:, e:e + 1], ALU.mult, ALU.add)\
                        .then_inc(s["conv"], 1)
                    for k in range(1, DC):
                        ve.wait_ge(s["conv"], n + DC * e + k)
                        ve.scalar_tensor_tensor(out=delta[:, e, :], in0=tmp_b[:, e, k:k + L], scalar=cw[:, e, k:k + 1],
                                                in1=delta[:, e, :], op0=ALU.mult, op1=ALU.add).then_inc(s["conv"], 1)
                ve.wait_ge(s["tz_ok"], bb + 1)
                ve.scalar_tensor_tensor(out=xn[:], in0=tmp_a[:], scalar=1.0, in1=xn[:], op0=ALU.add, op1=ALU.mult)\
                    .then_inc(s["gate_ok"], 1)
                for e in range(ET):
                    ve.wait_ge(s["tanh_u"], ET * bb + e + 1)
                    ve.scalar_tensor_tensor(out=du[:, e, :], in0=tmp_c[:, e, :], scalar=1.0, in1=delta[:, e, :],
                                            op0=ALU.add, op1=ALU.mult).then_inc(s["u_ok"], 1)
                ve.wait_ge(s["u_ok"], ET * (bb + 1))
                for e in range(ET):
                    ve.tensor_scalar(y2[:, e, 0, :], du[:, e, :], dhalf[:, e:e + 1], None, ALU.mult)
                ve.memset(y2[:, :, 1, :], 0.0).then_inc(s["y_init"], 1)
                ve.wait_ge(s["dtv_ok"], ET * (bb + 1))
                ve.wait_ge(s["e1_ok"], bb + 1)
                ve.tensor_scalar(delta[:], tb, 0.0, None, ALU.max).then_inc(s["relu_ok"], 1)
                ve.wait_ge(s["relu_ok"], bb + 1)
                ve.tensor_scalar(tb, tmp_a[:], 1.0, 1.0, ALU.add, ALU.subtract).then_inc(s["back_ok"], 1)
                ve.wait_ge(s["back_ok"], bb + 1)
                ve.tensor_tensor(tb, tmp_a[:], tb, ALU.subtract).then_inc(s["corr_ok"], 1)
                ve.wait_ge(s["corr_ok"], bb + 1)
                ve.wait_ge(s["ln_ok"], bb + 1)
                ve.tensor_tensor(tmp_c[:], tmp_c[:], tb, ALU.add).then_inc(s["sum1_ok"], 1)
                ve.wait_ge(s["sum1_ok"], bb + 1)
                ve.tensor_tensor(delta[:], delta[:], tmp_c[:], ALU.add).then_inc(s["delta_ok"], 1)
                ve.wait_ge(s["delta_ok"], bb + 1)
                ve.wait_ge(s["y_init"], bb + 1)
                ve.wait_ge(s["xproj_ok"], bb + 1)
                ve.scalar_tensor_tensor(out=du[:], in0=delta[:], scalar=0.5, in1=du[:], op0=ALU.mult, op1=ALU.mult)\
                    .then_inc(s["front_ok"], 1)

            def scan(gs, e):
                ve.wait_ge(s["da_ready"], gs + 1)
                ve.wait_ge(s["dbu_ready"], gs + 1)
                ve.tensor_tensor_scan(st[:, e % 2, :, :].rearrange("p n l -> p (n l)"),
                                      da[:, e % 2, :, :].rearrange("p n l -> p (n l)"),
                                      dbu[:, e % 2, :, :].rearrange("p n l -> p (n l)"),
                                      0.0, ALU.mult, ALU.add).then_inc(s["scan_done"], 1)

            def readout(gs, j, e):
                ve.wait_ge(s["scan_done"], gs + SEED + 1)
                ve.wait_ge(s["yadd_done"], gs + 1)
                ve.tensor_tensor(prod[:, e % 2, :, :], st[:, e % 2, :, :],
                                 bc[:, bass.ds(j % 2, 1), 2:4, :].rearrange("p o n l -> p (o n) l"), ALU.mult)\
                    .then_inc(s["prod_ready"], 1)

            def split_low(c, i):
                ve.wait_ge(s["prep_hi"], c + 1)
                ve.scalar_tensor_tensor(out=wring[:, i, HALF:2 * HALF], in0=w32[:, i % 2, :], scalar=WS,
                                        in1=wring[:, i, 0:HALF], op0=ALU.mult, op1=ALU.subtract)\
                    .then_inc(s["prep_lo"], 1)

            def link(bb):
                ve.wait_ge(s["yadd_done"], SL * (bb + 1) + SEED)
                ve.tensor_tensor(tmp_a[:], y2[:, :, 0, :], y2[:, :, 1, :], ALU.add).then_inc(s["ysum"], 1)
                ve.wait_ge(s["ysum"], bb + 1)
                ve.tensor_tensor(tmp_a[:], tmp_a[:], xn[:], ALU.mult).then_inc(s["yg"], 1)
                ve.wait_ge(s["yg"], bb + 1)
                ve.wait_ge(s["xt_in"], 16 * (bb + 1))
                ve.scalar_tensor_tensor(out=x1[:], in0=tmp_a[:], scalar=gates[:, 0:1], in1=xt[:], op0=ALU.mult,
                                        op1=ALU.add).then_inc(s["x1_ok"], 1)
                ve.wait_ge(s["mean_ok"], bb + 1)
                for e in range(ET):
                    last = ve.tensor_tensor(tb[:, e, :], x1[:, e, :], ps[0][:], ALU.subtract)
                last.then_inc(s["xc_ok"], 1)
                ve.wait_ge(s["rs_ok"], bb + 1)
                for e in range(ET):
                    last = ve.tensor_tensor(tb[:, e, :], tb[:, e, :], tmp_a[:, 1, :], ALU.mult)
                last.then_inc(s["xnorm"], 1)
                ve.wait_ge(s["xh_ok"], bb + 1)
                ve.wait_ge(s["xnorm"], bb + 1)
                ve.tensor_tensor(xl[:], tb, xh[:], ALU.subtract).then_inc(s["xl_ok"], 1)
                ve.wait_ge(s["logits"], bb + 1)
                ve.tensor_copy(lg[:, :, 0:R], ps[0][:, 0:64].rearrange("p (t c) -> p t c", t=ET)[:, :, 0:R])\
                    .then_inc(s["lg_ok"], 1)
                ve.wait_ge(s["lg_ok"], bb + 1)
                ve.memset(gap[:], 0.0)
                for t in range(ET):
                    last = ve.max(top[:, t, :], lg[:, t, 0:E])
                last.then_inc(s["top_ok"], 1)
                ve.wait_ge(s["top_ok"], bb + 1)
                ve.tensor_tensor(gap[:], top[:, :, 1], top[:, :, 0], ALU.subtract).then_inc(s["gap_ok"], 1)
                for t in range(ET):
                    last = ve.max_index(topi[:, t, :], top[:, t, :], lg[:, t, 0:E])
                last.then_inc(s["topi_ok"], 1)
                ve.wait_ge(s["topi_ok"], bb + 1)
                ve.tensor_copy(topf[:], topi[:, :, 0:2]).then_inc(s["topf_ok"], 1)
                ve.wait_ge(s["e2_ok"], bb + 1)
                ve.tensor_scalar(den[:], e2[:], 1.0, None, ALU.add).then_inc(s["den_ok"], 1)
                ve.wait_ge(s["den_ok"], bb + 1)
                ve.reciprocal(p1[:], den[:]).then_inc(s["p1_ok"], 1)
                ve.wait_ge(s["p1_ok"], bb + 1)
                ve.wait_ge(s["topf_ok"], bb + 1)
                ve.tensor_tensor(p2[:], p1[:], e2[:], ALU.mult).then_inc(s["p2_ok"], 1)
                ve.wait_ge(s["p2_ok"], bb + 1)
                for t in range(ET):
                    ve.tensor_scalar(hot[:, t, :], iota[:], topf[:, t, 0:1], p1[:, t:t + 1], ALU.is_equal, ALU.mult)
                    last = ve.tensor_scalar(hot2[:, t, :], iota[:], topf[:, t, 1:2], p2[:, t:t + 1], ALU.is_equal, ALU.mult)
                last.then_inc(s["hot_ok"], 1)
                ve.wait_ge(s["hot_ok"], bb + 1)
                ve.tensor_tensor(hot[:], hot[:], hot2[:], ALU.add).then_inc(s["sg_ok"], 1)
                ve.wait_ge(s["sg_ok"], bb + 1)
                ve.tensor_scalar(comb[:, :, 0:E], hot[:], HS / (2 * WS * WS), None, ALU.mult)
                ve.wait_ge(s["tsg"], bb + 1)
                for r in range(E, TROWS):
                    last = ve.tensor_scalar(comb[:, :, r], sg[:], 1.0, 0.5 * HS / (2 * WS * WS), ALU.add, ALU.mult)
                last.then_inc(s["comb_ok"], 1)

            def silu_gate(g):
                ve.wait_ge(s["tanh_done"], g + 1)
                ve.scalar_tensor_tensor(out=act_a, in0=th, scalar=1.0, in1=ps_g[:], op0=ALU.add, op1=ALU.mult)\
                    .then_inc(s["g_used"], 1)

            def hidden(g, i, hslot, scale_count):
                ve.wait_ge(s["g_used"], g + 2)
                ve.wait_ge(s["u_ready"], g + 1)
                ve.tensor_tensor(act_b, act_a, ps_u[:], ALU.mult).then_inc(s["u_used"], 1)
                ve.wait_ge(s["u_used"], g + 2)
                ve.wait_ge(scale_in[i], scale_count)
                ve.wait_ge(s["hlo_done"], g + 1)
                ve.tensor_tensor(hf[:, hslot, :], act_b, scale[:, i, :], ALU.mult).then_inc(s["hmul_done"], 1)

            def low(g, hslot):
                ve.wait_ge(s["hi_done"], g + 1)
                ve.tensor_tensor(hlo[:, hslot, :], hf[:, hslot, :], hhi[:, hslot, :], ALU.subtract)\
                    .then_inc(s["hlo_done"], 1)

            ve.memset(mean_w[:], 1.0 / DI).then_inc(s["const_dve"], 1)
            ve.memset(zeros16[:], 0.0).then_inc(s["const_dve"], 1)
            ve.memset(eps[:], EPS).then_inc(s["const_dve"], 1)
            ve.memset(one[:], 1.0).then_inc(s["const_dve"], 1)
            for e in range(E):
                ve.memset(iota[:, e:e + 1], float(e))
            for n in range(2):
                ve.memset(da[:, n, 1, 0:1], 0.0)
            at = 0
            for name, count in (("scan_done", SEED), ("yadd_done", SEED), ("hlo_done", SEED), ("down_done", SEED),
                                ("g_used", 1), ("u_used", 1), ("fin_ok", 1)):
                for n in range(count):
                    ve.memset(seedbox[:, at:at + 1], 0.0).then_inc(s[name], 1)
                    at += 1
            ve.wait_ge(s["consts"], 16 * 12)
            ve.wait_ge(s["const_act"], 2)
            ve.tensor_scalar(amat[:], amat[:], -1.0, None, ALU.mult).then_inc(s["const_dve2"], 1)
            ve.tensor_scalar(dhalf[:], dhalf[:], 0.5, None, ALU.mult).then_inc(s["const_dve2"], 1)
            ve.tensor_scalar(gates[:, 0:1], gates[:, 0:1], 0.5, None, ALU.mult)
            ve.tensor_scalar(gates[:, 1:2], gates[:, 1:2], 1.0 / (WS * HS), None, ALU.mult).then_inc(s["const_dve2"], 1)
            ve.wait_ge(s["const_dve2"], 3)
            front(0, True)
            with ve.Fori(0, NP) as j:
                ve.wait_ge(s["bc_in"], 16 * (j + 1))
                for i in range(4):
                    scan(4 * j + i, i)
                    split_low(4 * j + i, i)
                    readout(4 * j + i, j, i)
            split_low(CH - 1, 0)
            link(0)

            def scale_fills(i, upto):
                return sum(len(chunk_segments(c)) for c in range(i, upto, 4))

            def mixture(b, scan_next):
                for c in range(CH):
                    g = CH * b + c
                    i = c % 4
                    silu_gate(g)
                    on = scan_next and c < SL
                    if on:
                        if i == 0:
                            ve.wait_ge(s["bc_in"], 16 * (NP * (b + 1) + c // 4 + 1))
                        scan(SL * (b + 1) + c, i)
                    hidden(g, i, i % 2 if c < CH - 1 else 2, 16 * (scale_fills(i, CH) * b + scale_fills(i, c + 1)))
                    if on:
                        readout(SL * (b + 1) + c, c // 4, i)
                    low(g, i % 2 if c < CH - 1 else 2)
                ve.wait_ge(s["down_done"], CH * (b + 1) + SEED)
                for m in range(ET):
                    last = ve.scalar_tensor_tensor(out=tmp_a[:, m, :], in0=acc[:, m, :], scalar=gates[:, 1:2],
                                                   in1=x1[:, m, :], op0=ALU.mult, op1=ALU.add)
                last.then_inc(s["fin_ok"], 1)
                ve.wait_ge(s["out_done"], 16 * (b + 1))

            with ve.Fori(0, B - 1) as b:
                front(b + 1, False)
                mixture(b, True)
                link(b + 1)
            mixture(B - 1, False)

        @block.gpsimd
        def _(pool):
            def inject(gs, slot, e):
                pool.wait_ge(s["scan_done"], gs + 1)
                pool.tensor_tensor(dbu[:, e % 2, :, :], du[:, e:e + 1, :].broadcast_to([P, 2, L]),
                                   bc[:, slot, 0:2, :], ALU.mult).then_inc(s["dbu_ready"], 1)

            def add(gs, e):
                pool.wait_ge(s["prod_ready"], gs + 1)
                pool.tensor_tensor(y2[:, e, :, :], y2[:, e, :, :], prod[:, e % 2, :, :], ALU.add)\
                    .then_inc(s["yadd_done"], 1)

            def scan(bb):
                with pool.Fori(0, NP // 2) as jj:
                    pool.wait_ge(s["front_ok"], bb + 1)
                    for slot in range(2):
                        pool.wait_ge(s["bc_in"], 16 * (NP * bb + 2 * jj + slot + 1))
                        gs = SL * bb + 8 * jj + 4 * slot
                        inject(gs, slot, 0)
                        for i in range(1, 4):
                            inject(gs + i, slot, i)
                            add(gs + i - 1, i - 1)
                        add(gs + 3, 3)

            scan(0)
            with pool.Fori(1, B) as bb:
                scan(bb)


def kernel(x, ctx_1024, g_xattn, g_ffn, L0_xattn_in_proj_w, L0_xattn_conv_w, L0_xattn_conv_b, L0_xattn_x_proj_w,
           L0_xattn_dt_proj_w, L0_xattn_dt_proj_b, L0_xattn_A_log, L0_xattn_D, L0_ffn_router_weight,
           L0_ffn_gate_up_proj, L0_ffn_down_proj, L0_ffn_sh_gate_w, L0_ffn_sh_up_w, L0_ffn_sh_down_w,
           L0_ffn_shared_gate_w):
    import concourse.bacc as bacc
    from concourse.bass_utils import run_bass_kernel_spmd

    def tiles(a):
        return np.asarray(a).reshape(-1, P, a.shape[-1]).transpose(1, 0, 2)

    x = np.asarray(x)
    gu = np.asarray(L0_ffn_gate_up_proj)
    gate = np.concatenate([gu[:, :I_MOE].reshape(-1, DI), L0_ffn_sh_gate_w])
    up = np.concatenate([gu[:, I_MOE:].reshape(-1, DI), L0_ffn_sh_up_w])
    down = np.concatenate([np.asarray(L0_ffn_down_proj).transpose(0, 2, 1).reshape(-1, DI),
                           np.asarray(L0_ffn_sh_down_w).T])

    def by_chunk(w):
        return w.reshape(CH, P, ET, P).transpose(0, 3, 2, 1).reshape(CH, P, ET * P)

    arrays = {
        "x_nat": x.reshape(B, ET, P, L).transpose(0, 2, 1, 3),
        "x_t": x.transpose(0, 2, 1).reshape(B, ET, P, L).transpose(0, 2, 1, 3),
        "ctx_t": np.asarray(ctx_1024).transpose(0, 2, 1).reshape(B, KT, P, L).transpose(0, 2, 1, 3),
        "g_xattn": g_xattn,
        "g_ffn": g_ffn,
        "win_t": tiles(np.asarray(L0_xattn_in_proj_w).T),
        "conv_w": tiles(L0_xattn_conv_w),
        "conv_b": np.asarray(L0_xattn_conv_b).reshape(ET, P).T,
        "xproj_t": tiles(np.asarray(L0_xattn_x_proj_w).T),
        "dt_t": np.asarray(L0_xattn_dt_proj_w).T,
        "dt_b": np.asarray(L0_xattn_dt_proj_b).reshape(ET, P).T,
        "a_log": tiles(L0_xattn_A_log),
        "d_skip": np.asarray(L0_xattn_D).reshape(ET, P).T,
        "router_t": tiles(np.concatenate([L0_ffn_router_weight, L0_ffn_shared_gate_w]).T),
        "w_raw": np.concatenate([by_chunk(gate), by_chunk(up), down.reshape(CH, P, DI)], axis=2),
        "ident_in": np.eye(P, dtype=np.float32),
    }
    arrays = {k: np.ascontiguousarray(v) for k, v in arrays.items()}
    nc = bacc.Bacc("TRN2", target_bir_lowering=False, num_devices=1)
    aps = [nc.dram_tensor(k, v.shape, mybir.dt.from_np(v.dtype), kind="ExternalInput").ap() for k, v in arrays.items()]
    out = nc.dram_tensor("out_t", (B, P, ET, L), F32, kind="ExternalOutput").ap()
    program(nc, *aps, out)
    r = run_bass_kernel_spmd(nc, [arrays], core_ids=[0])
    got = r.results[0]["out_t"]
    return got.transpose(0, 3, 2, 1).reshape(B, L, DI)
```

```python
from contextlib import ExitStack

import numpy as np

import concourse.bass as bass
from concourse import mybir

ALU = mybir.AluOpType
ACT = mybir.ActivationFunctionType
F32 = mybir.dt.float32
F16 = mybir.dt.float16
U32 = mybir.dt.uint32

P = 128
B, L, DI = 4, 512, 512
DM = 256
DS, DC = 16, 4
DR = 16
E, I_MOE, I_SH = 8, 352, 1408
ET = DI // P
KT = DM // P
XD = DR + 2 * DS
NP = DS // 2
SL = NP * ET
CH = (E * I_MOE + I_SH) // P
SH_ROWS = I_SH // I_MOE
TROWS = E + SH_ROWS
R = E + 1
UPW = 2 * 512
DNW = 512
HALF = UPW + DNW
EPS = 1e-5
WS = 64.0
HS = 8.0
SEED = 2
RING = 3
C0 = 6
ROUNDS = CH // RING


def chunk_segments(c):
    row = c * P // I_MOE
    q = (row + 1) * I_MOE - c * P
    if q >= P:
        return [(0, P // 2, row), (P // 2, P, row)]
    return [(0, q, row), (q, P, row + 1)]


def program(nc, x_nat, x_t, ctx_t, g_xattn, g_ffn, win_t, conv_w, conv_b, xproj_t, dt_t, dt_b, a_log, d_skip,
            router_t, w_raw, ident_in, out):
    up_split = nc.dram_tensor("up_split", [CH, P, 2 * UPW], F16, kind="Internal").ap()
    down_split = nc.dram_tensor("down_split", [CH, P, 2 * DNW], F16, kind="Internal").ap()
    bc_dram = nc.dram_tensor("bc_dram", [2 * DS, L], F32, kind="Internal").ap()
    table_dram = nc.dram_tensor("table_dram", [TROWS, L], F32, kind="Internal").ap()

    with ExitStack() as ctx:
        def sb(name, shape, dt=F32):
            return ctx.enter_context(nc.sbuf_tensor(name, shape, dt))

        def psum(name, shape):
            return ctx.enter_context(nc.psum_tensor(name, shape, F32))

        def sem(name):
            return ctx.enter_context(nc.semaphore(name))

        win = sb("win", [P, KT, DI])
        cw = sb("cw", [P, ET, DC])
        cbias = sb("cbias", [P, ET])
        xproj = sb("xproj", [P, ET, XD])
        dtw = sb("dtw", [DR, DI])
        dtb = sb("dtb", [P, ET])
        amat = sb("amat", [P, ET, DS])
        dhalf = sb("dhalf", [P, ET])
        rout = sb("rout", [P, ET, R])
        ident = sb("ident", [P, P])
        mean_w = sb("mean_w", [P, P])
        zeros16 = sb("zeros16", [P, P], F16)
        gates = sb("gates", [P, 2])
        eps = sb("eps", [P, 1])
        one = sb("one", [P, 1])
        iota = sb("iota", [P, E])
        seedbox = sb("seedbox", [P, 16])
        ctxb = sb("ctxb", [P, KT, L])
        xn = sb("xn", [P, ET, L])
        xt = sb("xt", [P, ET, L])
        x1 = sb("x1", [P, ET, L])
        result = sb("result", [P, ET, L])
        xh = sb("xh", [P, ET, L], F16)
        xl = sb("xl", [P, ET, L], F16)
        tmp_a = sb("tmp_a", [P, ET, L])
        tmp_b = sb("tmp_b", [P, ET, 516])
        tmp_c = sb("tmp_c", [P, ET, L])
        tb = tmp_b[:, :, 0:L]
        du = sb("du", [P, ET, L])
        delta = sb("delta", [P, ET, L])
        y2 = sb("y2", [P, ET, 2, L])
        xdbl = sb("xdbl", [XD, L])
        stats = sb("stats", [P, ET, 6])
        mv = sb("mv", [P, ET, 2])
        lnv = sb("lnv", [P, ET])
        rstd = sb("rstd", [P, ET])
        lg = sb("lg", [P, ET, 16])
        carry = sb("carry", [P, 1])
        top = sb("top", [P, ET, 8])
        topi = sb("topi", [P, ET, 8], U32)
        topf = sb("topf", [P, ET, 2])
        gap = sb("gap", [P, ET])
        e2 = sb("e2", [P, ET])
        den = sb("den", [P, ET])
        p1 = sb("p1", [P, ET])
        p2 = sb("p2", [P, ET])
        sg = sb("sg", [P, ET])
        hot = sb("hot", [P, ET, E])
        hot2 = sb("hot2", [P, ET, E])
        comb = sb("comb", [P, ET, TROWS])
        combt = sb("combt", [TROWS, L])
        bc = sb("bc", [P, 2, 4, L])
        da = sb("da", [P, 2, 2, L])
        dbu = sb("dbu", [P, 2, 2, L])
        st = sb("st", [P, 2, 2, L])
        prod = sb("prod", [P, 2, 2, L])
        wup = sb("wup", [P, RING, 2 * UPW], F16)
        wdown = sb("wdown", [P, RING, 2 * DNW], F16)
        scale = sb("scale", [P, RING, L])
        mbuf = sb("mbuf", [P, 6, L])
        w32 = mbuf[:, :, :].rearrange("p (s a) l -> p s (a l)", s=2)
        th, act_a, act_b = mbuf[:, 0, :], mbuf[:, 1, :], mbuf[:, 2, :]
        hf = mbuf[:, 3:6, :]
        hhi = sb("hhi", [P, RING, L], F16)
        hlo = sb("hlo", [P, RING, L], F16)

        acc = psum("acc", [P, ET, L])
        ps_g = psum("ps_g", [P, L])
        ps_u = psum("ps_u", [P, L])
        ps = [psum("ps_0", [P, L]), psum("ps_1", [P, L])]

        names = """consts seeds const_dve const_act const_dve2
            ctx_in xn_in xt_in bn_stats bn_aggr ln1 rstd_ok z_ok tz_ok gate_ok inproj xp_ok pads conv tanh_u u_ok
            xproj_ok xdbl_ok bc_stored dt_ok dtv_ok abs_ok e1_ok ln_ok relu_ok back_ok corr_ok sum1_ok delta_ok y_init
            front_ok bc_in da_ready dbu_ready scan_done prod_ready yadd_done
            ysum yg x1_ok mean_ok xc_ok sq_ok var_ok ln2 rs_ok xnorm xh_ok xl_ok logits lg_ok top_ok topi_ok topf_ok
            gap_ok e2_ok den_ok p1_ok p2_ok hot_ok comb_ok tsg sg_ok combt_ps combt_ok table_ok
            g_ready u_ready g_used u_used tanh_done hmul_done hi_done hlo_done down_done open_ok fin_ok out_done
            prep_hi prep_lo x1_copied""".split()
        s = {n: sem(n) for n in names}
        raw_in = [sem(f"raw_in{i}") for i in range(2)]
        stored = [sem(f"stored{i}") for i in range(2)]
        up_in = [sem(f"up_in{i}") for i in range(RING)]
        down_in = [sem(f"down_in{i}") for i in range(RING)]
        scale_in = [sem(f"scale_in{i}") for i in range(RING)]

        block = ctx.enter_context(nc.Block())

        @block.sync
        def _(sp):
            def row_of(dram, bb):
                return dram[bass.ds(bb, 1)].rearrange("b p k l -> p (b k) l")

            def load_ctx(bb, first):
                if not first:
                    sp.wait_ge(s["inproj"], ET * bb)
                sp.dma_start(ctxb[:], row_of(ctx_t, bb)).then_inc(s["ctx_in"], 16)

            def load_xn(bb, first):
                if not first:
                    sp.wait_ge(s["yg"], ET * bb)
                sp.dma_start(xn[:], row_of(x_nat, bb)).then_inc(s["xn_in"], 16)

            def load_xt(bb, first):
                if not first:
                    sp.wait_ge(s["x1_copied"], bb)
                sp.dma_start(xt[:], row_of(x_t, bb)).then_inc(s["xt_in"], 16)

            def store_bc(bb):
                sp.wait_ge(s["xdbl_ok"], bb + 1)
                sp.dma_start(bc_dram, xdbl[DR:XD, :]).then_inc(s["bc_stored"], 16)
                sp.wait_ge(s["bc_stored"], 16 * (bb + 1))

            def load_bc(bb, t, first=False):
                if not first:
                    sp.wait_ge(s["bc_in"], 16 * (NP * bb + t))
                src = bass.AP(bc_dram.tensor, 2 * L * t, [[0, P], [DS * L, 2], [1, 2 * L]])
                sp.dma_start(bc[:, bass.ds(t % 2, 1), :, :].rearrange("p o (a n) l -> p (o a) (n l)", a=2), src)\
                    .then_inc(s["bc_in"], 16)

            def bc_slot_free(bb, t):
                sp.wait_ge(s["prod_ready"], SL * bb + ET * (t - 1))
                sp.wait_ge(s["dbu_ready"], SL * bb + ET * (t - 1))

            def load_raw(c, slot):
                sp.dma_start(w32[:, slot, :], w_raw[bass.ds(c, 1)].rearrange("c p n -> p (c n)")).then_inc(raw_in[slot], 16)

            def store_split(c, slot):
                sp.wait_ge(s["prep_lo"], c + 1)
                sp.dma_start(up_split[bass.ds(c, 1)].rearrange("c p n -> p (c n)"), wup[:, slot, :])\
                    .then_inc(stored[slot], 16)
                sp.dma_start(down_split[bass.ds(c, 1)].rearrange("c p n -> p (c n)"), wdown[:, slot, :])\
                    .then_inc(stored[slot], 16)

            for dst, src in (
                (win[:], win_t), (cw[:], conv_w), (cbias[:], conv_b), (xproj[:], xproj_t), (dtw[:], dt_t),
                (dtb[:], dt_b), (amat[:], a_log), (dhalf[:], d_skip), (rout[:], router_t), (ident[:], ident_in),
                (gates[:, 0:1], bass.AP(g_xattn.tensor, 0, [[0, P], [1, 1]])),
                (gates[:, 1:2], bass.AP(g_ffn.tensor, 0, [[0, P], [1, 1]])),
            ):
                sp.dma_start(dst, src).then_inc(s["consts"], 16)
            load_ctx(0, True)
            load_xn(0, True)
            load_xt(0, True)
            load_raw(0, 0)
            load_raw(1, 1)
            store_bc(0)
            load_bc(0, 0, True)
            load_bc(0, 1)
            with sp.Fori(0, NP - 2) as t:
                for i in range(4):
                    store_split(4 * t + i, i % 2)
                    load_raw(4 * t + i + 2, i % 2)
                bc_slot_free(0, t + 2)
                load_bc(0, t + 2)
            for c in range(4 * (NP - 2), CH):
                store_split(c, c % 2)
                if c + 2 < CH:
                    load_raw(c + 2, c % 2)
            sp.wait_ge(stored[0], 32 * (CH // 2 + 1))
            sp.wait_ge(stored[1], 32 * (CH // 2))

            def load_up(c):
                sp.dma_start(wup[:, c % RING, :], up_split[c]).then_inc(up_in[c % RING], 16)

            def load_down(c):
                sp.dma_start(wdown[:, c % RING, :], down_split[c]).then_inc(down_in[c % RING], 16)

            def load_scale(c):
                for p, q, row in chunk_segments(c):
                    src = bass.AP(table_dram.tensor, L * row, [[0, q - p], [1, L]])
                    sp.dma_start(scale[p:q, c % RING, :], src).then_inc(scale_in[c % RING], 16)

            def mixture(b, beside):
                if beside:
                    load_ctx(b + 1, False)
                    load_xn(b + 1, False)
                sp.wait_ge(s["combt_ok"], b + 1)
                sp.dma_start(table_dram, combt[:, :]).then_inc(s["table_ok"], 16)
                sp.wait_ge(s["table_ok"], 16 * (b + 1))
                load_scale(0)
                load_scale(1)
                if beside:
                    load_xt(b + 1, False)
                for c in range(CH):
                    g = CH * b + c
                    t = (c - C0) // RING
                    if beside and c > C0 and (c - C0) % RING == 0 and t + 1 < NP:
                        bc_slot_free(b + 1, t + 1)
                        load_bc(b + 1, t + 1)
                    if c + 2 < CH:
                        if c > 0:
                            sp.wait_ge(s["hmul_done"], g)
                        load_scale(c + 2)
                    nxt = (c + RING) % CH
                    if c + RING < CH or beside:
                        sp.wait_ge(s["u_ready"], g + 1)
                        load_up(nxt)
                        sp.wait_ge(s["down_done"], g + 1)
                        load_down(nxt)
                    if beside and c == 1:
                        store_bc(b + 1)
                        load_bc(b + 1, 0, True)
                        load_bc(b + 1, 1)
                sp.wait_ge(s["fin_ok"], b + 2)
                sp.dma_start(row_of(out, b), result[:]).then_inc(s["out_done"], 16)

            for c in range(RING):
                load_up(c)
                load_down(c)
            with sp.Fori(0, B - 1) as b:
                mixture(b, True)
            mixture(B - 1, False)
            sp.wait_ge(s["out_done"], 16 * B + 1)

        @block.tensor
        def _(pe):
            def in_projection(bb, first):
                if not first:
                    pe.wait_ge(s["combt_ok"], bb)
                pe.wait_ge(s["ctx_in"], 16 * (bb + 1))
                for e in range(ET):
                    if e >= 2:
                        pe.wait_ge(s["xp_ok"], ET * bb + e - 1)
                    for k in range(KT):
                        last = pe.matmul(ps[e % 2][:], win[:, k, e * P:(e + 1) * P], ctxb[:, k, :],
                                         start=(k == 0), stop=(k == KT - 1))
                    last.then_inc(s["inproj"], 1)

            def x_projection(bb):
                pe.wait_ge(s["xp_ok"], ET * bb + ET)
                for e in range(ET):
                    pe.wait_ge(s["u_ok"], ET * bb + e + 1)
                    last = pe.matmul(ps[0][0:XD, :], xproj[:, e, :], du[:, e, :], start=(e == 0), stop=(e == ET - 1))
                last.then_inc(s["xproj_ok"], 1)

            def dt_projection(bb):
                pe.wait_ge(s["xdbl_ok"], bb + 1)
                for e in range(ET):
                    if e >= 2:
                        pe.wait_ge(s["dtv_ok"], ET * bb + e - 1)
                    pe.matmul(ps[e % 2][:], dtw[:, e * P:(e + 1) * P], xdbl[0:DR, :], start=True, stop=True)\
                        .then_inc(s["dt_ok"], 1)

            def mean(bb):
                pe.wait_ge(s["dtv_ok"], ET * (bb + 1))
                for e in range(ET):
                    pe.wait_ge(s["x1_ok"], ET * bb + e + 1)
                    last = pe.matmul(ps[0][:], mean_w[:], xt[:, e, :], start=(e == 0), stop=(e == ET - 1))
                last.then_inc(s["mean_ok"], 1)

            def variance(bb):
                for e in range(ET):
                    pe.wait_ge(s["sq_ok"], ET * bb + e + 1)
                    last = pe.matmul(ps[1][:], mean_w[:], tmp_c[:, e, :], start=(e == 0), stop=(e == ET - 1))
                last.then_inc(s["var_ok"], 1)

            def router(bb):
                pe.wait_ge(s["xnorm"], ET * (bb + 1))
                for t in range(ET):
                    for e in range(ET):
                        last = pe.matmul(ps[0][:, t * 16:t * 16 + R], tb[:, e, t * P:(t + 1) * P], rout[:, e, :],
                                         start=(e == 0), stop=(e == ET - 1))
                last.then_inc(s["logits"], 1)

            def turn_table(bb):
                pe.wait_ge(s["comb_ok"], bb + 1)
                for t in range(ET):
                    last = pe.transpose(ps[1][0:TROWS, t * P:(t + 1) * P], comb[:, t, :], ident[:])
                last.then_inc(s["combt_ps"], 1)

            def up(g, slot, count):
                pe.wait_ge(up_in[slot], count)
                for part, bank, used, ready in ((0, ps_g, "g_used", "g_ready"), (1, ps_u, "u_used", "u_ready")):
                    pe.wait_ge(s[used], g + 1)
                    n = 0
                    for k in range(ET):
                        for low, rhs in ((0, xh), (0, xl), (1, xh)):
                            at = UPW * low + 512 * part + P * k
                            last = pe.matmul(bank[:], wup[:, slot, at:at + P], rhs[:, k, :],
                                             start=(n == 0), stop=(n == 3 * ET - 1))
                            n += 1
                    last.then_inc(s[ready], 1)

            def down(g, slot, count, closing=False):
                pe.wait_ge(down_in[slot], count)
                pe.wait_ge(s["hlo_done"], g + 1)
                for m in range(ET):
                    for n, (low, rhs) in enumerate(((0, hhi), (0, hlo), (1, hhi))):
                        at = DNW * low + P * m
                        last = pe.matmul(acc[:, m, :], wdown[:, slot, at:at + P], rhs[:, slot, :],
                                         start=False, stop=(closing and n == 2), skip_group_check=True)
                last.then_inc(s["down_done"], 1)

            def mixture(b, beside):
                def up_of(c):
                    up(CH * b + c, c % RING, 16 * (ROUNDS * b + c // RING + 1))

                def down_of(c):
                    down(CH * b + c, c % RING, 16 * (ROUNDS * b + c // RING + 1), closing=(c == CH - 1))

                pe.wait_ge(s["xl_ok"], ET * (b + 1))
                up_of(0)
                if beside:
                    in_projection(b + 1, False)
                up_of(1)
                pe.wait_ge(s["fin_ok"], b + 1)
                for m in range(ET):
                    pe.matmul(acc[:, m, :], zeros16[:], xh[:, m, :], start=True, stop=False, skip_group_check=True)
                down_of(0)
                for c in range(1, C0):
                    up_of(c + 1)
                    down_of(c)
                    if beside and c == 1:
                        x_projection(b + 1)
                    if beside and c == 2:
                        dt_projection(b + 1)
                with pe.Fori(0, NP) as t:
                    for i in range(RING):
                        c = C0 + RING * t + i
                        up(CH * b + c + 1, (i + 1) % RING, 16 * (ROUNDS * b + C0 // RING + t + (i + 1) // RING + 1))
                        down(CH * b + c, i, 16 * (ROUNDS * b + C0 // RING + t + 1))
                if beside:
                    mean(b + 1)
                up_of(CH - 2)
                down_of(CH - 3)
                if beside:
                    variance(b + 1)
                up_of(CH - 1)
                down_of(CH - 2)
                if beside:
                    router(b + 1)
                down_of(CH - 1)
                if beside:
                    turn_table(b + 1)

            pe.wait_ge(s["consts"], 16 * 12)
            pe.wait_ge(s["const_dve"], 4)
            in_projection(0, True)
            x_projection(0)
            dt_projection(0)
            mean(0)
            variance(0)
            router(0)
            turn_table(0)
            with pe.Fori(0, B - 1) as b:
                mixture(b, True)
            mixture(B - 1, False)

        @block.scalar
        def _(act):
            def row_rstd(bb):
                act.wait_ge(s["bn_aggr"], ET * (bb + 1))
                act.activation(lnv[:], mv[:, :, 1], ACT.Ln, bias=eps[:, 0:1]).then_inc(s["ln1"], 1)
                act.wait_ge(s["ln1"], bb + 1)
                act.activation(rstd[:], lnv[:], ACT.Exp, scale=-0.5).then_inc(s["rstd_ok"], 1)

            def projected(bb):
                act.wait_ge(s["pads"], bb + 1)
                for e in range(ET):
                    act.wait_ge(s["inproj"], ET * bb + e + 1)
                    act.activation(tmp_b[:, e, DC - 1:DC - 1 + L], ps[e % 2][:], ACT.Copy).then_inc(s["xp_ok"], 1)

            def squash_conv(bb):
                for e in range(ET):
                    act.wait_ge(s["conv"], DC * (ET * bb + e + 1))
                    act.activation(tmp_c[:, e, :], delta[:, e, :], ACT.Tanh, scale=0.5).then_inc(s["tanh_u"], 1)

            def squash_z(bb):
                act.wait_ge(s["z_ok"], ET * (bb + 1))
                act.activation(tmp_a[:], xn[:], ACT.Tanh, scale=0.5).then_inc(s["tz_ok"], 1)

            def x_rows(bb):
                act.wait_ge(s["xproj_ok"], bb + 1)
                act.activation(xdbl[:], ps[0][0:XD, :], ACT.Copy, scale=0.5).then_inc(s["xdbl_ok"], 1)

            def dt_rows(bb):
                for e in range(ET):
                    act.wait_ge(s["dt_ok"], ET * bb + e + 1)
                    act.activation(tb[:, e, :], ps[e % 2][:], ACT.Identity, bias=dtb[:, e:e + 1])\
                        .then_inc(s["dtv_ok"], 1)
                act.wait_ge(s["dtv_ok"], ET * (bb + 1))
                act.wait_ge(s["gate_ok"], bb + 1)
                act.activation(tmp_a[:], tb, ACT.Abs).then_inc(s["abs_ok"], 1)
                act.wait_ge(s["abs_ok"], bb + 1)
                act.activation(tmp_a[:], tmp_a[:], ACT.Exp, scale=-1.0).then_inc(s["e1_ok"], 1)

            def log_rows(bb):
                act.wait_ge(s["e1_ok"], bb + 1)
                act.activation(tmp_c[:], tmp_a[:], ACT.Ln, bias=one[:, 0:1]).then_inc(s["ln_ok"], 1)
                act.activation(lnv[:], rstd[:], ACT.Exp)

            def decay(gs, t, e):
                act.wait_ge(s["scan_done"], gs + 1)
                act.activation(da[:, e % 2, 0, :], delta[:, e, :], ACT.Exp, scale=amat[:, e, bass.ds(2 * t, 1)])
                act.activation(da[:, e % 2, 1, 1:L], delta[:, e, 1:L], ACT.Exp, scale=amat[:, e, bass.ds(2 * t + 1, 1)])\
                    .then_inc(s["da_ready"], 1)

            def squares(bb):
                for e in range(ET):
                    act.wait_ge(s["xc_ok"], ET * bb + e + 1)
                    act.activation(tmp_c[:, e, :], tb[:, e, :], ACT.Square).then_inc(s["sq_ok"], 1)

            def token_rstd(bb):
                act.wait_ge(s["var_ok"], bb + 1)
                act.activation(tmp_a[:, 0, :], ps[1][:], ACT.Ln, bias=eps[:, 0:1]).then_inc(s["ln2"], 1)
                act.wait_ge(s["ln2"], bb + 1)
                act.activation(tmp_a[:, 1, :], tmp_a[:, 0, :], ACT.Exp, scale=-0.5).then_inc(s["rs_ok"], 1)

            def x_high(bb, first):
                if not first:
                    act.wait_ge(s["u_ready"], CH * bb)
                for e in range(ET):
                    act.wait_ge(s["xnorm"], ET * bb + e + 1)
                    act.activation(xh[:, e, :], tb[:, e, :], ACT.Copy).then_inc(s["xh_ok"], 1)

            def router_exps(bb):
                act.wait_ge(s["gap_ok"], bb + 1)
                act.activation(e2[:], gap[:], ACT.Exp).then_inc(s["e2_ok"], 1)
                act.activation(sg[:], lg[:, :, E], ACT.Tanh, scale=0.5).then_inc(s["tsg"], 1)
                act.wait_ge(s["combt_ps"], bb + 1)
                act.activation(combt[:], ps[1][0:TROWS, :], ACT.Copy).then_inc(s["combt_ok"], 1)

            def squash(g):
                act.wait_ge(s["g_ready"], g + 1)
                act.activation(th, ps_g[:], ACT.Tanh, scale=0.5 / WS).then_inc(s["tanh_done"], 1)

            def high(g, slot):
                act.wait_ge(s["hmul_done"], g + 1)
                act.activation(hhi[:, slot, :], hf[:, slot, :], ACT.Copy).then_inc(s["hi_done"], 1)

            def split(i):
                act.activation(wup[:, i, 0:UPW], w32[:, i, 0:UPW], ACT.Copy, scale=WS)
                act.activation(wdown[:, i, 0:DNW], w32[:, i, UPW:HALF], ACT.Copy, scale=WS).then_inc(s["prep_hi"], 1)

            act.wait_ge(s["consts"], 16 * 12)
            act.activation(amat[:], amat[:], ACT.Exp).then_inc(s["const_act"], 1)
            act.activation(gates[:], gates[:], ACT.Tanh).then_inc(s["const_act"], 1)
            act.wait_ge(s["const_dve"], 4)
            act.wait_ge(s["const_dve2"], 3)
            row_rstd(0)
            projected(0)
            squash_conv(0)
            squash_z(0)
            x_rows(0)
            dt_rows(0)
            log_rows(0)
            act.wait_ge(s["front_ok"], 1)
            for i in range(4):
                act.wait_ge(raw_in[i % 2], 16 * (i // 2 + 1))
                decay(i, 0, i)
                if i >= 2:
                    act.wait_ge(stored[i % 2], 32)
                split(i % 2)
            with act.Fori(1, NP) as t:
                for i in range(4):
                    decay(4 * t + i, t, i)
                    act.wait_ge(raw_in[i % 2], 16 * (2 * t + i // 2 + 1))
                    act.wait_ge(stored[i % 2], 32 * (2 * t + i // 2))
                    split(i % 2)
            act.wait_ge(raw_in[0], 16 * (CH // 2 + 1))
            act.wait_ge(stored[0], 32 * (CH // 2))
            split(0)
            squares(0)
            token_rstd(0)
            x_high(0, True)
            router_exps(0)

            def mixture(b, beside):
                def both(c):
                    squash(CH * b + c)
                    high(CH * b + c, c % RING)

                if beside:
                    row_rstd(b + 1)
                both(0)
                if beside:
                    projected(b + 1)
                    squash_conv(b + 1)
                both(1)
                if beside:
                    squash_z(b + 1)
                both(2)
                if beside:
                    x_rows(b + 1)
                both(3)
                if beside:
                    dt_rows(b + 1)
                both(4)
                if beside:
                    log_rows(b + 1)
                both(5)
                if beside:
                    act.wait_ge(s["front_ok"], b + 2)
                with act.Fori(0, NP) as t:
                    g = CH * b + C0 + RING * t
                    gs = SL * (b + 1) + 4 * t
                    if beside:
                        decay(gs, t, 0)
                        decay(gs + 1, t, 1)
                    squash(g)
                    high(g, 0)
                    if beside:
                        decay(gs + 2, t, 2)
                    squash(g + 1)
                    if beside:
                        decay(gs + 3, t, 3)
                    high(g + 1, 1)
                    squash(g + 2)
                    high(g + 2, 2)
                both(CH - 3)
                if beside:
                    squares(b + 1)
                both(CH - 2)
                if beside:
                    token_rstd(b + 1)
                both(CH - 1)
                if beside:
                    x_high(b + 1, False)
                    router_exps(b + 1)

            with act.Fori(0, B - 1) as b:
                mixture(b, True)
            mixture(B - 1, False)

        @block.vector
        def _(ve):
            def row_stats(bb):
                ve.wait_ge(s["xn_in"], 16 * (bb + 1))
                for e in range(ET):
                    ve.bn_stats(stats[:, e, :], xn[:, e, :]).then_inc(s["bn_stats"], 1)
                ve.wait_ge(s["bn_stats"], ET * (bb + 1))
                ve.memset(tmp_b[:, :, 0:DC - 1], 0.0).then_inc(s["pads"], 1)
                for e in range(ET):
                    ve.bn_aggr(mv[:, e, :], stats[:, e, :]).then_inc(s["bn_aggr"], 1)

            def convolution(bb):
                n = DC * ET * bb
                for e in range(ET):
                    ve.wait_ge(s["xp_ok"], ET * bb + e + 1)
                    ve.tensor_scalar(delta[:, e, :], tmp_b[:, e, 0:L], cw[:, e, 0:1], cbias[:, e:e + 1], ALU.mult, ALU.add)\
                        .then_inc(s["conv"], 1)
                    for k in range(1, DC):
                        ve.wait_ge(s["conv"], n + DC * e + k)
                        ve.scalar_tensor_tensor(out=delta[:, e, :], in0=tmp_b[:, e, k:k + L], scalar=cw[:, e, k:k + 1],
                                                in1=delta[:, e, :], op0=ALU.mult, op1=ALU.add).then_inc(s["conv"], 1)

            def normed_rows(bb):
                ve.wait_ge(s["rstd_ok"], bb + 1)
                for e in range(ET):
                    ve.tensor_scalar(xn[:, e, :], xn[:, e, :], mv[:, e, 0:1], rstd[:, e:e + 1], ALU.subtract, ALU.mult)\
                        .then_inc(s["z_ok"], 1)

            def silu_u(bb):
                for e in range(ET):
                    ve.wait_ge(s["tanh_u"], ET * bb + e + 1)
                    ve.scalar_tensor_tensor(out=du[:, e, :], in0=tmp_c[:, e, :], scalar=1.0, in1=delta[:, e, :],
                                            op0=ALU.add, op1=ALU.mult).then_inc(s["u_ok"], 1)
                ve.wait_ge(s["u_ok"], ET * (bb + 1))
                for e in range(ET):
                    ve.tensor_scalar(y2[:, e, 0, :], du[:, e, :], dhalf[:, e:e + 1], None, ALU.mult)
                ve.memset(y2[:, :, 1, :], 0.0).then_inc(s["y_init"], 1)

            def silu_z(bb):
                ve.wait_ge(s["tz_ok"], bb + 1)
                ve.scalar_tensor_tensor(out=xn[:], in0=tmp_a[:], scalar=1.0, in1=xn[:], op0=ALU.add, op1=ALU.mult)\
                    .then_inc(s["gate_ok"], 1)

            def softplus_rest(bb):
                ve.wait_ge(s["dtv_ok"], ET * (bb + 1))
                ve.tensor_scalar(delta[:], tb, 0.0, None, ALU.max).then_inc(s["relu_ok"], 1)
                ve.wait_ge(s["relu_ok"], bb + 1)
                ve.wait_ge(s["e1_ok"], bb + 1)
                ve.tensor_scalar(tb, tmp_a[:], 1.0, 1.0, ALU.add, ALU.subtract).then_inc(s["back_ok"], 1)
                ve.wait_ge(s["back_ok"], bb + 1)
                ve.tensor_tensor(tb, tmp_a[:], tb, ALU.subtract).then_inc(s["corr_ok"], 1)

            def softplus_sum(bb):
                ve.wait_ge(s["corr_ok"], bb + 1)
                ve.tensor_tensor(delta[:], delta[:], tb, ALU.add).then_inc(s["sum1_ok"], 1)
                ve.wait_ge(s["sum1_ok"], bb + 1)
                ve.wait_ge(s["ln_ok"], bb + 1)
                ve.tensor_tensor(delta[:], delta[:], tmp_c[:], ALU.add).then_inc(s["delta_ok"], 1)
                ve.wait_ge(s["delta_ok"], bb + 1)
                ve.wait_ge(s["y_init"], bb + 1)
                ve.wait_ge(s["xproj_ok"], bb + 1)
                ve.scalar_tensor_tensor(out=du[:], in0=delta[:], scalar=0.5, in1=du[:], op0=ALU.mult, op1=ALU.mult)\
                    .then_inc(s["front_ok"], 1)

            def scan(gs, e):
                ve.wait_ge(s["da_ready"], gs + 1)
                ve.wait_ge(s["dbu_ready"], gs + 1)
                ve.tensor_tensor_scan(st[:, e % 2, :, :].rearrange("p n l -> p (n l)"),
                                      da[:, e % 2, :, :].rearrange("p n l -> p (n l)"),
                                      dbu[:, e % 2, :, :].rearrange("p n l -> p (n l)"),
                                      0.0, ALU.mult, ALU.add).then_inc(s["scan_done"], 1)

            def readout(gs, t, e):
                ve.wait_ge(s["scan_done"], gs + SEED + 1)
                ve.wait_ge(s["yadd_done"], gs + 1)
                ve.tensor_tensor(prod[:, e % 2, :, :], st[:, e % 2, :, :],
                                 bc[:, bass.ds(t % 2, 1), 2:4, :].rearrange("p o n l -> p (o n) l"), ALU.mult)\
                    .then_inc(s["prod_ready"], 1)

            def split_low(c, i):
                ve.wait_ge(s["prep_hi"], c + 1)
                ve.scalar_tensor_tensor(out=wup[:, i, UPW:2 * UPW], in0=w32[:, i, 0:UPW], scalar=WS,
                                        in1=wup[:, i, 0:UPW], op0=ALU.mult, op1=ALU.subtract)
                ve.scalar_tensor_tensor(out=wdown[:, i, DNW:2 * DNW], in0=w32[:, i, UPW:HALF], scalar=WS,
                                        in1=wdown[:, i, 0:DNW], op0=ALU.mult, op1=ALU.subtract)\
                    .then_inc(s["prep_lo"], 1)

            def first_residual(bb):
                for e in range(ET):
                    ve.wait_ge(s["yadd_done"], SL * (bb + 1) + SEED - ET + e + 1)
                    ve.tensor_tensor(tmp_a[:, e, :], y2[:, e, 0, :], y2[:, e, 1, :], ALU.add).then_inc(s["ysum"], 1)
                for e in range(ET):
                    ve.wait_ge(s["ysum"], ET * bb + e + 1)
                    ve.tensor_tensor(tmp_a[:, e, :], tmp_a[:, e, :], xn[:, e, :], ALU.mult).then_inc(s["yg"], 1)
                for e in range(ET):
                    ve.wait_ge(s["yg"], ET * bb + e + 1)
                    if e == 0:
                        ve.wait_ge(s["xt_in"], 16 * (bb + 1))
                    ve.scalar_tensor_tensor(out=xt[:, e, :], in0=tmp_a[:, e, :], scalar=gates[:, 0:1], in1=xt[:, e, :],
                                            op0=ALU.mult, op1=ALU.add).then_inc(s["x1_ok"], 1)

            def centre(bb):
                ve.wait_ge(s["mean_ok"], bb + 1)
                for e in range(ET):
                    ve.tensor_tensor(tb[:, e, :], xt[:, e, :], ps[0][:], ALU.subtract).then_inc(s["xc_ok"], 1)

            def normed(bb):
                ve.wait_ge(s["rs_ok"], bb + 1)
                ve.wait_ge(s["sq_ok"], ET * (bb + 1))
                for e in range(ET):
                    ve.tensor_tensor(tb[:, e, :], tb[:, e, :], tmp_a[:, 1, :], ALU.mult).then_inc(s["xnorm"], 1)

            def x_low(bb):
                for e in range(ET):
                    ve.wait_ge(s["xh_ok"], ET * bb + e + 1)
                    ve.tensor_tensor(xl[:, e, :], tb[:, e, :], xh[:, e, :], ALU.subtract).then_inc(s["xl_ok"], 1)

            def route(bb):
                ve.wait_ge(s["logits"], bb + 1)
                ve.tensor_copy(lg[:, :, 0:R], ps[0][:, 0:64].rearrange("p (t c) -> p t c", t=ET)[:, :, 0:R])\
                    .then_inc(s["lg_ok"], 1)
                ve.wait_ge(s["lg_ok"], bb + 1)
                ve.memset(carry[:], 0.0)
                for t in range(ET):
                    last = ve.max(top[:, t, :], lg[:, t, 0:E])
                last.then_inc(s["top_ok"], 1)
                ve.wait_ge(s["top_ok"], bb + 1)
                ve.tensor_tensor(gap[:], top[:, :, 1], top[:, :, 0], ALU.subtract).then_inc(s["gap_ok"], 1)
                for t in range(ET):
                    last = ve.max_index(topi[:, t, :], top[:, t, :], lg[:, t, 0:E])
                last.then_inc(s["topi_ok"], 1)
                ve.wait_ge(s["topi_ok"], bb + 1)
                ve.tensor_copy(topf[:], topi[:, :, 0:2]).then_inc(s["topf_ok"], 1)
                ve.wait_ge(s["e2_ok"], bb + 1)
                ve.tensor_scalar(den[:], e2[:], 1.0, None, ALU.add).then_inc(s["den_ok"], 1)
                ve.wait_ge(s["den_ok"], bb + 1)
                ve.reciprocal(p1[:], den[:]).then_inc(s["p1_ok"], 1)
                ve.wait_ge(s["p1_ok"], bb + 1)
                ve.wait_ge(s["topf_ok"], bb + 1)
                ve.tensor_tensor(p2[:], p1[:], e2[:], ALU.mult).then_inc(s["p2_ok"], 1)
                ve.wait_ge(s["p2_ok"], bb + 1)
                for t in range(ET):
                    ve.tensor_scalar(hot[:, t, :], iota[:], topf[:, t, 0:1], p1[:, t:t + 1], ALU.is_equal, ALU.mult)
                    last = ve.tensor_scalar(hot2[:, t, :], iota[:], topf[:, t, 1:2], p2[:, t:t + 1], ALU.is_equal, ALU.mult)
                last.then_inc(s["hot_ok"], 1)
                ve.wait_ge(s["hot_ok"], bb + 1)
                ve.tensor_tensor(hot[:], hot[:], hot2[:], ALU.add).then_inc(s["sg_ok"], 1)
                ve.wait_ge(s["sg_ok"], bb + 1)
                ve.tensor_scalar(comb[:, :, 0:E], hot[:], HS / (2 * WS * WS), None, ALU.mult)
                ve.wait_ge(s["tsg"], bb + 1)
                for r in range(E, TROWS):
                    last = ve.tensor_scalar(comb[:, :, r], sg[:], 1.0, 0.5 * HS / (2 * WS * WS), ALU.add, ALU.mult)
                last.then_inc(s["comb_ok"], 1)

            def silu_gate(g):
                ve.wait_ge(s["tanh_done"], g + 1)
                ve.scalar_tensor_tensor(out=act_a, in0=th, scalar=1.0, in1=ps_g[:], op0=ALU.add, op1=ALU.mult)\
                    .then_inc(s["g_used"], 1)

            def hidden(g, slot, scale_count):
                ve.wait_ge(s["g_used"], g + 2)
                ve.wait_ge(s["u_ready"], g + 1)
                ve.tensor_tensor(act_b, act_a, ps_u[:], ALU.mult).then_inc(s["u_used"], 1)
                ve.wait_ge(s["u_used"], g + 2)
                ve.wait_ge(scale_in[slot], scale_count)
                ve.tensor_tensor(hf[:, slot, :], act_b, scale[:, slot, :], ALU.mult).then_inc(s["hmul_done"], 1)

            def low(g, slot):
                ve.wait_ge(s["hi_done"], g + 1)
                ve.tensor_tensor(hlo[:, slot, :], hf[:, slot, :], hhi[:, slot, :], ALU.subtract)\
                    .then_inc(s["hlo_done"], 1)

            ve.memset(mean_w[:], 1.0 / DI).then_inc(s["const_dve"], 1)
            ve.memset(zeros16[:], 0.0).then_inc(s["const_dve"], 1)
            ve.memset(eps[:], EPS).then_inc(s["const_dve"], 1)
            ve.memset(one[:], 1.0).then_inc(s["const_dve"], 1)
            for e in range(E):
                ve.memset(iota[:, e:e + 1], float(e))
            for n in range(2):
                ve.memset(da[:, n, 1, 0:1], 0.0)
            at = 0
            for name, count in (("scan_done", SEED), ("yadd_done", SEED), ("g_used", 1), ("u_used", 1), ("fin_ok", 1),
                                ("out_done", 1)):
                for n in range(count):
                    ve.memset(seedbox[:, at:at + 1], 0.0).then_inc(s[name], 1)
                    at += 1
            ve.wait_ge(s["consts"], 16 * 12)
            ve.wait_ge(s["const_act"], 2)
            ve.tensor_scalar(amat[:], amat[:], -1.0, None, ALU.mult).then_inc(s["const_dve2"], 1)
            ve.tensor_scalar(dhalf[:], dhalf[:], 0.5, None, ALU.mult).then_inc(s["const_dve2"], 1)
            ve.tensor_scalar(gates[:, 0:1], gates[:, 0:1], 0.5, None, ALU.mult)
            ve.tensor_scalar(gates[:, 1:2], gates[:, 1:2], 1.0 / (WS * HS), None, ALU.mult).then_inc(s["const_dve2"], 1)
            ve.wait_ge(s["const_dve2"], 3)
            row_stats(0)
            convolution(0)
            silu_u(0)
            normed_rows(0)
            silu_z(0)
            softplus_rest(0)
            softplus_sum(0)
            with ve.Fori(0, NP) as t:
                ve.wait_ge(s["bc_in"], 16 * (t + 1))
                for i in range(4):
                    scan(4 * t + i, i)
                    split_low(4 * t + i, i % 2)
                    readout(4 * t + i, t, i)
            split_low(CH - 1, 0)
            first_residual(0)
            centre(0)
            normed(0)
            x_low(0)
            route(0)
            ve.tensor_copy(x1[:], xt[:]).then_inc(s["x1_copied"], 1)

            def mixture(b, beside):
                def chunk(c):
                    silu_gate(CH * b + c)
                    hidden(CH * b + c, c % RING, 32 * (ROUNDS * b + c // RING + 1))
                    low(CH * b + c, c % RING)

                if beside:
                    row_stats(b + 1)
                chunk(0)
                if beside:
                    convolution(b + 1)
                chunk(1)
                if beside:
                    silu_u(b + 1)
                    normed_rows(b + 1)
                chunk(2)
                if beside:
                    silu_z(b + 1)
                chunk(3)
                if beside:
                    softplus_rest(b + 1)
                chunk(4)
                if beside:
                    softplus_sum(b + 1)
                chunk(5)
                with ve.Fori(0, NP) as t:
                    g = CH * b + C0 + RING * t
                    gs = SL * (b + 1) + 4 * t
                    count = 32 * (ROUNDS * b + C0 // RING + t + 1)
                    if beside:
                        ve.wait_ge(s["bc_in"], 16 * (NP * (b + 1) + t + 1))
                    for i, (inner, after) in enumerate(((0, None), (1, 2), (3, None))):
                        silu_gate(g + i)
                        if beside:
                            scan(gs + inner, inner)
                        hidden(g + i, i, count)
                        if beside:
                            readout(gs + inner, t, inner)
                        low(g + i, i)
                        if beside and after is not None:
                            scan(gs + after, after)
                            readout(gs + after, t, after)
                if beside:
                    first_residual(b + 1)
                chunk(CH - 3)
                if beside:
                    centre(b + 1)
                chunk(CH - 2)
                if beside:
                    normed(b + 1)
                chunk(CH - 1)
                if beside:
                    x_low(b + 1)
                    route(b + 1)
                ve.wait_ge(s["out_done"], 16 * b + 1)
                ve.wait_ge(s["down_done"], CH * (b + 1))
                for m in range(ET):
                    last = ve.scalar_tensor_tensor(out=result[:, m, :], in0=acc[:, m, :], scalar=gates[:, 1:2],
                                                   in1=x1[:, m, :], op0=ALU.mult, op1=ALU.add)
                last.then_inc(s["fin_ok"], 1)
                if beside:
                    ve.wait_ge(s["fin_ok"], b + 2)
                    ve.tensor_copy(x1[:], xt[:]).then_inc(s["x1_copied"], 1)

            with ve.Fori(0, B - 1) as b:
                mixture(b, True)
            mixture(B - 1, False)

        @block.gpsimd
        def _(pool):
            def inject(gs, slot, e):
                pool.wait_ge(s["scan_done"], gs + 1)
                pool.tensor_tensor(dbu[:, e % 2, :, :], du[:, e:e + 1, :].broadcast_to([P, 2, L]),
                                   bc[:, slot, 0:2, :], ALU.mult).then_inc(s["dbu_ready"], 1)

            def add(gs, e):
                pool.wait_ge(s["prod_ready"], gs + 1)
                pool.tensor_tensor(y2[:, e, :, :], y2[:, e, :, :], prod[:, e % 2, :, :], ALU.add)\
                    .then_inc(s["yadd_done"], 1)

            def pair(bb, t, slot, start):
                pool.wait_ge(s["bc_in"], 16 * (NP * bb + t + 1))
                gs = SL * bb + 4 * t
                inject(gs, slot, 0)
                if not start:
                    add(gs - 1, 3)
                for i in range(1, 4):
                    inject(gs + i, slot, i)
                    add(gs + i - 1, i - 1)

            def scan(bb):
                pool.wait_ge(s["front_ok"], bb + 1)
                pair(bb, 0, 0, True)
                pair(bb, 1, 1, False)
                with pool.Fori(1, NP // 2) as tt:
                    pair(bb, 2 * tt, 0, False)
                    pair(bb, 2 * tt + 1, 1, False)
                add(SL * bb + SL - 1, 3)

            scan(0)
            with pool.Fori(1, B) as bb:
                scan(bb)


def kernel(x, ctx_1024, g_xattn, g_ffn, L0_xattn_in_proj_w, L0_xattn_conv_w, L0_xattn_conv_b, L0_xattn_x_proj_w,
           L0_xattn_dt_proj_w, L0_xattn_dt_proj_b, L0_xattn_A_log, L0_xattn_D, L0_ffn_router_weight,
           L0_ffn_gate_up_proj, L0_ffn_down_proj, L0_ffn_sh_gate_w, L0_ffn_sh_up_w, L0_ffn_sh_down_w,
           L0_ffn_shared_gate_w):
    import concourse.bacc as bacc
    from concourse.bass_utils import run_bass_kernel_spmd

    def tiles(a):
        return np.asarray(a).reshape(-1, P, a.shape[-1]).transpose(1, 0, 2)

    x = np.asarray(x)
    gu = np.asarray(L0_ffn_gate_up_proj)
    gate = np.concatenate([gu[:, :I_MOE].reshape(-1, DI), L0_ffn_sh_gate_w])
    up = np.concatenate([gu[:, I_MOE:].reshape(-1, DI), L0_ffn_sh_up_w])
    down = np.concatenate([np.asarray(L0_ffn_down_proj).transpose(0, 2, 1).reshape(-1, DI),
                           np.asarray(L0_ffn_sh_down_w).T])

    def by_chunk(w):
        return w.reshape(CH, P, ET, P).transpose(0, 3, 2, 1).reshape(CH, P, ET * P)

    arrays = {
        "x_nat": x.reshape(B, ET, P, L).transpose(0, 2, 1, 3),
        "x_t": x.transpose(0, 2, 1).reshape(B, ET, P, L).transpose(0, 2, 1, 3),
        "ctx_t": np.asarray(ctx_1024).transpose(0, 2, 1).reshape(B, KT, P, L).transpose(0, 2, 1, 3),
        "g_xattn": g_xattn,
        "g_ffn": g_ffn,
        "win_t": tiles(np.asarray(L0_xattn_in_proj_w).T),
        "conv_w": tiles(L0_xattn_conv_w),
        "conv_b": np.asarray(L0_xattn_conv_b).reshape(ET, P).T,
        "xproj_t": tiles(np.asarray(L0_xattn_x_proj_w).T),
        "dt_t": np.asarray(L0_xattn_dt_proj_w).T,
        "dt_b": np.asarray(L0_xattn_dt_proj_b).reshape(ET, P).T,
        "a_log": tiles(L0_xattn_A_log),
        "d_skip": np.asarray(L0_xattn_D).reshape(ET, P).T,
        "router_t": tiles(np.concatenate([L0_ffn_router_weight, L0_ffn_shared_gate_w]).T),
        "w_raw": np.concatenate([by_chunk(gate), by_chunk(up), down.reshape(CH, P, DI)], axis=2),
        "ident_in": np.eye(P, dtype=np.float32),
    }
    arrays = {k: np.ascontiguousarray(v) for k, v in arrays.items()}
    nc = bacc.Bacc("TRN2", target_bir_lowering=False, num_devices=1)
    aps = [nc.dram_tensor(k, v.shape, mybir.dt.from_np(v.dtype), kind="ExternalInput").ap() for k, v in arrays.items()]
    out = nc.dram_tensor("out_t", (B, P, ET, L), F32, kind="ExternalOutput").ap()
    program(nc, *aps, out)
    r = run_bass_kernel_spmd(nc, [arrays], core_ids=[0])
    got = r.results[0]["out_t"]
    return got.transpose(0, 3, 2, 1).reshape(B, L, DI)
```

```python
from contextlib import ExitStack

import numpy as np

import concourse.bass as bass
from concourse import mybir

ALU = mybir.AluOpType
ACT = mybir.ActivationFunctionType
AX = mybir.AxisListType
F32 = mybir.dt.float32
F16 = mybir.dt.float16
U32 = mybir.dt.uint32
I32 = mybir.dt.int32

P = 128
B, L, DI = 4, 512, 512
DM = 256
DS, DC = 16, 4
DR = 16
E, I_MOE, I_SH = 8, 352, 1408
ET = DI // P
KT = DM // P
XD = DR + 2 * DS
NP = DS // 2
SL = NP * ET
CH = I_SH // P
TT = B * ET
NT = 2 * TT + E - 1
KH = -(-I_MOE // P)
HP = KH * P
R = E + 1
UPW = 2 * 512
DNW = 512
HALF = UPW + DNW
XUP = ET * 2 * I_MOE
XDN = KH * DI
XW = 2 * (XUP + XDN)
PIECES = 3 * E
EPS = 1e-5
WS = 64.0
HS = 8.0
HC = HS / (2 * WS * WS)
EARLY = 3
AT_ONCE = 6
SEED = 2
C0 = 2
S_OF = ((CH + 1) // 2, CH // 2)


def program(nc, x_nat, x_t, ctx_t, g_xattn, g_ffn, win_t, conv_w, conv_b, xproj_t, dt_t, dt_b, a_log, d_skip,
            router_t, w_raw, x_up, x_down, ident_in, ident16_in, tri_in, steps_in, index_in, token_in, out):
    up_split = nc.dram_tensor("up_split", [CH, P, 2 * UPW], F16, kind="Internal").ap()
    down_split = nc.dram_tensor("down_split", [CH, P, 2 * DNW], F16, kind="Internal").ap()
    bc_dram = nc.dram_tensor("bc_dram", [2 * DS, L], F32, kind="Internal").ap()
    x16_dram = nc.dram_tensor("x16_dram", [TT * P, 2 * DI], F16, kind="Internal").ap()
    base_dram = nc.dram_tensor("base_dram", [B, P, ET, DI], F32, kind="Internal").ap()
    list_dram = nc.dram_tensor("list_dram", [NT * P, 1], I32, kind="Internal").ap()
    y_dram = nc.dram_tensor("y_dram", [NT * P, DI], F32, kind="Internal").ap()

    with ExitStack() as ctx:
        def sb(name, shape, dt=F32):
            return ctx.enter_context(nc.sbuf_tensor(name, shape, dt))

        def psum(name, shape):
            return ctx.enter_context(nc.psum_tensor(name, shape, F32))

        def sem(name):
            return ctx.enter_context(nc.semaphore(name))

        land = sb("land", [P, E * XW // 2])
        taken = [0]

        def carve(cols):
            taken[0] += cols
            assert taken[0] <= E * XW // 2
            return land[:, taken[0] - cols:taken[0]]

        def tiles_of(cols, n=ET):
            return carve(n * cols).rearrange("p (e l) -> p e l", e=n)

        def pair_slots():
            return carve(4 * L).rearrange("p (s n l) -> p s n l", s=2, n=2)

        da, dbu, st, prod = pair_slots(), pair_slots(), pair_slots(), pair_slots()
        bc = carve(8 * L).rearrange("p (s n l) -> p s n l", s=2, n=4)
        du = tiles_of(L)
        delta = tiles_of(L)
        ctxb = tiles_of(L, KT)
        win = tiles_of(DI, KT)
        y2 = carve(2 * ET * L).rearrange("p (e n l) -> p e n l", e=ET, n=2)
        xn = tiles_of(L)
        xt = tiles_of(L)
        tmp_a = tiles_of(L)
        tmp_b = tiles_of(516)
        tmp_c = tiles_of(L)
        tb = tmp_b[:, :, 0:L]
        xdbl = carve(L)[0:XD, :]
        dtw = carve(DI)[0:DR, :]
        xproj = tiles_of(XD)
        rout = tiles_of(R)
        xp = land[:, 4 * 2 * L:4 * 2 * L + ET * 516].rearrange("p (e l) -> p e l", e=ET)
        vt = dbu.rearrange("p s n l -> p (s n) l")
        wall = land[:].bitcast(F16).rearrange("p (e n) -> p e n", e=E)
        y_of = [land[:, k * TT * DI:(k + 1) * TT * DI].rearrange("p (t n) -> p t n", t=TT) for k in range(3)]
        cw = sb("cw", [P, ET, DC])
        cbias = sb("cbias", [P, ET])
        dtb = sb("dtb", [P, ET])
        amat = sb("amat", [P, ET, DS])
        dhalf = sb("dhalf", [P, ET])
        ident = sb("ident", [P, P])
        ident16 = sb("ident16", [P, P], F16)
        tri = sb("tri", [P, P], F16)
        ones16 = sb("ones16", [P, P], F16)
        zeros16 = sb("zeros16", [P, P], F16)
        mean_w = sb("mean_w", [P, P])
        gates = sb("gates", [P, 3])
        eps = sb("eps", [P, 1])
        one = sb("one", [P, 1])
        seedbox = sb("seedbox", [P, 16])
        steps = sb("steps", [P, E, TT])
        index = sb("index", [P, NT, E])
        xh = sb("xh", [P, ET, L], F16)
        xl = sb("xl", [P, ET, L], F16)
        stats = sb("stats", [P, ET, 6])
        mv = sb("mv", [P, ET, 2])
        lnv = sb("lnv", [P, ET])
        rstd = sb("rstd", [P, ET])
        lg = sb("lg", [P, ET, 16])
        carry = sb("carry", [P, 1])
        top = sb("top", [P, ET, 8])
        topi = sb("topi", [P, ET, 8], U32)
        gap = sb("gap", [P, ET])
        e2 = sb("e2", [P, ET])
        den = sb("den", [P, ET])
        p1 = sb("p1", [P, ET])
        sg = sb("sg", [P, ET])
        sgt = sb("sgt", [P, ET])
        choice = sb("choice", [P, 2, TT])
        weight = sb("weight", [P, 2, TT])
        hot = sb("hot", [P, 2, E, TT])
        count16 = sb("count16", [P, E * TT], F16)
        keep = sb("keep", [P, E, TT])
        totals = sb("totals", [P, E, TT])
        upto = sb("upto", [P, E, TT])
        place = sb("place", [P, E, TT])
        more = sb("more", [P, E, TT])
        ntiles = sb("ntiles", [P, E])
        tend = sb("tend", [P, E])
        first = sb("first", [P, E])
        posf = sb("posf", [P, 2, TT])
        pos = sb("pos", [P, 2, TT], I32)
        past = sb("past", [P, NT, E])
        tidf = sb("tidf", [P, NT])
        tid = sb("tid", [P, NT], I32)
        token = sb("token", [P, TT], I32)
        rows_i = sb("rows_i", [NT, P], I32)
        rows_f = sb("rows_f", [NT, P])
        listed = sb("listed", [P, NT], I32)
        x1tok = sb("x1tok", [P, ET, DI])
        xst = sb("xst", [P, ET, 2 * DI], F16)
        wup = sb("wup", [P, 2, 2 * UPW], F16)
        wdown = sb("wdown", [P, 2, 2 * DNW], F16)
        w32 = sb("w32", [P, 2, HALF])
        mbuf = sb("mbuf", [P, 3, L])
        th, act_a, hf = mbuf[:, 0, :], mbuf[:, 1, :], mbuf[:, 2, :]
        hhi = sb("hhi", [P, 2, L], F16)
        hlo = sb("hlo", [P, 2, L], F16)
        prod_pe = w32[:, :, 0:2 * L].rearrange("p s (n l) -> p s n l", n=2)
        xgt = wup[:, 0, :].rearrange("p (s n) -> p s n", s=2)
        ht = wup[:, 1, 0:4 * HP].rearrange("p (s n) -> p s n", s=2)
        yout = wdown[:, :, :].bitcast(F32)

        acc = psum("acc", [P, ET, L])
        ps_g = psum("ps_g", [P, L])
        ps_u = psum("ps_u", [P, L])
        ps = [psum("ps_0", [P, L]), psum("ps_1", [P, L])]

        names = """consts win_in const_dve const_act const_dve2 zeroed
            ctx_in xn_in xt_in bn_stats bn_aggr ln1 rstd_ok z_ok tz_ok gate_ok inproj xp_ok pads conv tanh_u u_ok
            xproj_ok xdbl_ok bc_stored dt_ok dtv_ok e1_ok ln_ok x_ok corr_ok delta_ok y_init
            front_ok da_ready dbu_ready scan_done prod_ready y_pe y_dve y_pool y_zero
            ysum yg x1_ok mean_ok xc_ok sq_ok var_ok ln2 rs_ok xnorm xh_ok xl_ok logits lg_ok top_ok topi_ok
            gap_ok e2_ok den_ok p1_ok tsg sgt_ok x1_ps x1tok_ok x16_ps x16_ok x16_stored
            g_ready u_ready g_used u_used tanh_done hi_done hlo_done down_done fin_ok base_out
            prep_hi prep_lo experts_hi experts_lo hot_ok prefix_ok assigned scattered listed_in rows_ok list_ps listed_ok
            xt_ps xt_ok eg_ready eu_ready etanh_done egs_done eh_done ehi_done elo_done ht_ps ht_ok edown_done y_ok
            base_in late_in first_sum summed out_done""".split()
        s = {n: sem(n) for n in names}
        raw_in = [sem(f"raw_in{i}") for i in range(2)]
        stored = [sem(f"stored{i}") for i in range(2)]
        bc_in = [sem(f"bc_in{i}") for i in range(2)]
        up_in = [sem(f"up_in{i}") for i in range(2)]
        down_in = [sem(f"down_in{i}") for i in range(2)]
        early_in = [sem(f"early_in{i}") for i in range(EARLY)]
        list_in = [sem(f"list_in{i}") for i in range(2)]
        y_out = [sem(f"y_out{i}") for i in range(2)]
        gathered = [sem(f"gathered{i}") for i in range(TT // 2)]
        ps_y = (ps_g, ps_u)
        NCONST = 16 * 16
        ASSIGN = 15

        def fills(row, c):
            return S_OF[c % 2] * row + c // 2 + 1

        def piece(j):
            e, r = j // 3, j % 3
            src, cols, at, step = ((x_up[2 * e + r], XUP // 2, r * XUP // 2, XUP) if r < 2 else
                                   (x_down[e], XDN, 2 * XUP, XDN))
            if e < EARLY:
                raw = land[:, (e + 1) * XW // 2:(e + 2) * XW // 2][:, r * XUP // 2:r * XUP // 2 + cols]
            else:
                raw = w32[:, j % 2, 0:cols]
            return e, src, cols, at, step, raw

        def arrived(engine, j):
            if j // 3 < EARLY:
                engine.wait_ge(early_in[j // 3], 48)
            else:
                engine.wait_ge(raw_in[j % 2], 16 * (S_OF[j % 2] + (j - (3 * EARLY + (j - 3 * EARLY) % 2)) // 2 + 1))

        def base_tile(t):
            if t < 2:
                return y_of[2][:, t, :]
            if t < 4:
                return xl[:, 2 * (t - 2):2 * (t - 1), :].bitcast(F32).rearrange("p a n -> p (a n)")
            if t < 6:
                return w32[:, t - 4, 2 * L:3 * L]
            if t < 8:
                return xh[:, 2 * (t - 6):2 * (t - 5), :].bitcast(F32).rearrange("p a n -> p (a n)")
            if t < 12:
                return w32[:, (t - 8) // 2, (t % 2) * L:(t % 2 + 1) * L]
            return x1tok[:, t - 12, :]

        beside_chunk = [2, 3, 3, 3, 2, 2, 2, 2, 2, 2, 1]
        split_by = [sum(beside_chunk[:c + 1]) for c in range(CH)]
        assert split_by[-1] == PIECES

        y_bank0 = [ps[0][:], ps[1][:], acc[:, 2, :], acc[:, 3, :]]
        last_order = list(range(2, TT)) + [0, 1]

        block = ctx.enter_context(nc.Block())

        @block.sync
        def _(sp):
            def row_of(dram, bb):
                return dram[bass.ds(bb, 1)].rearrange("b p k l -> p (b k) l")

            def load_ctx(bb, first):
                if not first:
                    sp.wait_ge(s["inproj"], ET * bb)
                sp.dma_start(ctxb[:], row_of(ctx_t, bb)).then_inc(s["ctx_in"], 16)

            def load_xn(bb, first):
                if not first:
                    sp.wait_ge(s["yg"], ET * bb)
                sp.dma_start(xn[:], row_of(x_nat, bb)).then_inc(s["xn_in"], 16)

            def load_xt(bb, first):
                if not first:
                    sp.wait_ge(s["x1_ps"], ET * bb)
                sp.dma_start(xt[:], row_of(x_t, bb)).then_inc(s["xt_in"], 16)

            def store_bc(bb):
                sp.wait_ge(s["xdbl_ok"], bb + 1)
                sp.dma_start(bc_dram, xdbl[DR:XD, :]).then_inc(s["bc_stored"], 16)
                sp.wait_ge(s["bc_stored"], 16 * (bb + 1))

            def load_bc(bb, t, slot, slot_taken=False):
                if slot_taken:
                    sp.wait_ge(s["prod_ready"], SL * bb + ET * (t - 1))
                    sp.wait_ge(s["dbu_ready"], SL * bb + ET * (t - 1))
                src = bass.AP(bc_dram.tensor, 2 * L * t, [[0, P], [DS * L, 2], [1, 2 * L]])
                sp.dma_start(bc[:, slot, :, :].rearrange("p (a n) l -> p a (n l)", a=2), src).then_inc(bc_in[slot], 16)

            def load_raw(c, slot):
                sp.dma_start(w32[:, slot, :], w_raw[bass.ds(c, 1)].rearrange("c p n -> p (c n)")).then_inc(raw_in[slot], 16)

            def store_split(c, slot):
                sp.wait_ge(s["prep_lo"], c + 1)
                sp.dma_start(up_split[bass.ds(c, 1)].rearrange("c p n -> p (c n)"), wup[:, slot, :])\
                    .then_inc(stored[slot], 16)
                sp.dma_start(down_split[bass.ds(c, 1)].rearrange("c p n -> p (c n)"), wdown[:, slot, :])\
                    .then_inc(stored[slot], 16)

            sp.dma_start(win[:], win_t).then_inc(s["win_in"], 16)
            load_ctx(0, True)
            for dst, src in (
                 (cw[:], conv_w), (cbias[:], conv_b), (xproj[:], xproj_t), (dtw[:], dt_t),
                (dtb[:], dt_b), (amat[:], a_log), (dhalf[:], d_skip), (rout[:], router_t), (ident[:], ident_in),
                (ident16[:], ident16_in), (tri[:], tri_in), (steps[:], steps_in), (index[:], index_in),
                (token[:], token_in),
                (gates[:, 0:1], bass.AP(g_xattn.tensor, 0, [[0, P], [1, 1]])),
                (gates[:, 1:2], bass.AP(g_ffn.tensor, 0, [[0, P], [1, 1]])),
            ):
                sp.dma_start(dst, src).then_inc(s["consts"], 16)
            load_xn(0, True)
            load_xt(0, True)
            load_raw(0, 0)
            load_raw(1, 1)
            store_split(0, 0)
            load_raw(2, 0)
            store_bc(0)
            load_bc(0, 0, 0)
            load_bc(0, 1, 1)
            load_ctx(1, False)
            sp.wait_ge(s["const_dve"], 6)
            sp.dma_start(list_dram.rearrange("(p t) o -> p (t o)", p=P), listed[:]).then_inc(s["zeroed"], 16)
            with sp.Fori(0, NP // 2 - 1) as tt:
                for i in range(2):
                    store_split(2 * tt + 1 + i, (1 + i) % 2)
                    load_raw(2 * tt + 3 + i, (1 + i) % 2)
                    load_bc(0, 2 * tt + i + 2, i, slot_taken=True)
            for c in range(NP - 1, CH):
                if c == NP + 1:
                    load_xn(1, False)
                store_split(c, c % 2)
                if c + 2 < CH:
                    load_raw(c + 2, c % 2)
            sp.wait_ge(stored[0], 32 * S_OF[0])
            sp.wait_ge(stored[1], 32 * S_OF[1])

            def load_up(c):
                sp.dma_start(wup[:, c % 2, :], up_split[c]).then_inc(up_in[c % 2], 16)

            def load_down(c):
                sp.dma_start(wdown[:, c % 2, :], down_split[c]).then_inc(down_in[c % 2], 16)

            def load_piece(j):
                e, src, cols, at, step, raw = piece(j)
                sp.dma_start(raw, src).then_inc(early_in[e] if e < EARLY else raw_in[j % 2], 16)

            def store_x16(bb):
                sp.wait_ge(s["x16_ok"], ET * (bb + 1))
                sp.dma_start(x16_dram.rearrange("(b t p) n -> b p t n", b=B, t=ET)[bass.ds(bb, 1)]
                             .rearrange("b p t n -> p (b t) n"), xst[:]).then_inc(s["x16_stored"], 16)

            def shared(b, beside, ahead=False):
                if ahead:
                    load_ctx(b + 2, False)
                store_x16(b)
                if beside:
                    load_xt(b + 1, False)
                for c in range(CH):
                    g = CH * b + c
                    t = c - C0
                    if beside and t >= 1 and t + 1 < NP:
                        load_bc(b + 1, t + 1, (t + 1) % 2, slot_taken=True)
                    if c + 2 < CH:
                        sp.wait_ge(s["u_ready"], g + 1)
                        load_up(c + 2)
                    pieces = range(split_by[c - 1] + 2 if c else 0, split_by[c] + 2) if not beside else []
                    pieces = [j for j in pieces if 3 * EARLY + 2 <= j < PIECES]
                    for j in pieces[:1]:
                        next_piece(j)
                    if c + 2 < CH:
                        sp.wait_ge(s["down_done"], g + 1)
                        load_down(c + 2)
                    for j in pieces[1:]:
                        next_piece(j)
                    if not beside and c == 0:
                        for j in range(AT_ONCE, 3 * EARLY + 2):
                            load_piece(j)
                if beside:
                    sp.wait_ge(s["down_done"], CH * (b + 1))
                    for c in range(2):
                        load_up(c)
                        load_down(c)
                    if ahead:
                        load_xn(b + 2, False)
                    sp.wait_ge(s["fin_ok"], b + 2)
                    sp.dma_start(row_of(base_dram, b), x1tok[:]).then_inc(s["base_out"], 16)
                    if ahead:
                        store_bc(b + 2)
                        load_bc(b + 2, 0, 0)
                        load_bc(b + 2, 1, 1)

            def next_piece(j):
                sp.wait_ge(s["experts_lo"], j - 1)
                load_piece(j)

            for c in range(2):
                load_up(c)
                load_down(c)
            store_bc(1)
            load_bc(1, 0, 0)
            load_bc(1, 1, 1)
            with sp.Fori(0, B - 2) as b:
                shared(b, True, True)
            shared(B - 2, True)
            sp.wait_ge(s["scan_done"], SL * B + SEED)
            sp.wait_ge(s["y_pe"], SL + 2 * NP * (B - 1) + SEED)
            sp.wait_ge(s["y_dve"], NP * (B - 1) + 1)
            sp.wait_ge(s["y_pool"], NP * (B - 1) + 1)
            for j in range(AT_ONCE):
                load_piece(j)
            shared(B - 1, False)

            def store_y(i, slot):
                sp.wait_ge(s["y_ok"], i + 1)
                sp.dma_start(y_dram.rearrange("(t p) n -> t p n", p=P)[bass.ds(i, 1)].rearrange("t p n -> p (t n)"),
                             yout[:, slot, :]).then_inc(y_out[slot], 16)

            sp.wait_ge(s["base_out"], 16 * (B - 1) + 1)
            sp.wait_ge(s["u_ready"], CH * B)
            sp.wait_ge(s["experts_lo"], PIECES)
            for t in range(2, TT - ET):
                sp.dma_start(base_tile(t), base_dram[t // ET][:, t % ET, :]).then_inc(s["base_in"], 16)
            with sp.Fori(0, NT // 2) as t:
                store_y(2 * t, 0)
                store_y(2 * t + 1, 1)
            store_y(NT - 1, 0)
            sp.wait_ge(s["edown_done"], NT)
            for t in range(2):
                sp.dma_start(base_tile(t), base_dram[0][:, t, :]).then_inc(s["late_in"], 16)
            for n, t in enumerate(last_order):
                sp.wait_ge(s["summed"], n // 2 + 1)
                sp.dma_start(out[t // ET, (t % ET) * P:(t % ET + 1) * P, :], base_tile(t)).then_inc(s["out_done"], 16)
            sp.wait_ge(s["out_done"], 16 * TT)

        @block.tensor
        def _(pe):
            def in_projection(bb, first, tiles):
                if 0 in tiles:
                    if not first:
                        pe.wait_ge(s["g_used"], CH * (bb - 1) + 1)
                        pe.wait_ge(s["u_used"], CH * (bb - 1) + 1)
                    pe.wait_ge(s["ctx_in"], 16 * (bb + 1))
                for e in tiles:
                    if e >= 2:
                        pe.wait_ge(s["xp_ok"], ET * bb + e - 1)
                    for k in range(KT):
                        last = pe.matmul(ps_y[e % 2][:], win[:, k, e * P:(e + 1) * P], ctxb[:, k, :],
                                         start=(k == 0), stop=(k == KT - 1))
                    last.then_inc(s["inproj"], 1)

            def x_projection(bb):
                pe.wait_ge(s["xp_ok"], ET * bb + ET)
                for e in range(ET):
                    pe.wait_ge(s["u_ok"], ET * bb + e + 1)
                    last = pe.matmul(ps_y[0][0:XD, :], xproj[:, e, :], du[:, e, :], start=(e == 0), stop=(e == ET - 1))
                last.then_inc(s["xproj_ok"], 1)

            def dt_projection(bb, tiles=range(ET)):
                pe.wait_ge(s["xdbl_ok"], bb + 1)
                for e in tiles:
                    if e >= 2:
                        pe.wait_ge(s["dtv_ok"], ET * bb + e - 1)
                    pe.matmul(ps_y[e % 2][:], dtw[:, e * P:(e + 1) * P], xdbl[0:DR, :], start=True, stop=True)\
                        .then_inc(s["dt_ok"], 1)

            def y_add(gs, slots, slot, bank, start=False):
                pe.wait_ge(s["prod_ready"], gs + 1)
                for n in range(2):
                    last = pe.matmul(bank, ident[:], slots[:, slot, n, :], start=(start and n == 0), stop=False,
                                     skip_group_check=True)
                last.then_inc(s["y_pe"], 1)

            def mean(bb):
                pe.wait_ge(s["dtv_ok"], ET * (bb + 1))
                for e in range(ET):
                    pe.wait_ge(s["x1_ok"], ET * bb + e + 1)
                    last = pe.matmul(ps[0][:], mean_w[:], xt[:, e, :], start=(e == 0), stop=(e == ET - 1))
                last.then_inc(s["mean_ok"], 1)

            def variance(bb):
                for e in range(ET):
                    pe.wait_ge(s["sq_ok"], ET * bb + e + 1)
                    last = pe.matmul(ps[1][:], mean_w[:], tmp_c[:, e, :], start=(e == 0), stop=(e == ET - 1))
                last.then_inc(s["var_ok"], 1)

            def router(bb):
                pe.wait_ge(s["xnorm"], ET * (bb + 1))
                for t in range(ET):
                    for e in range(ET):
                        last = pe.matmul(ps[0][:, t * 16:t * 16 + R], tb[:, e, t * P:(t + 1) * P], rout[:, e, :],
                                         start=(e == 0), stop=(e == ET - 1))
                last.then_inc(s["logits"], 1)

            def turn(bb, tiles):
                if 0 in tiles:
                    pe.wait_ge(s["lg_ok"], bb + 1)
                    pe.wait_ge(s["xl_ok"], ET * (bb + 1))
                rows = ps[0][:].bitcast(F16)
                for t in tiles:
                    if t > 0:
                        pe.wait_ge(s["x1tok_ok"], ET * bb + t)
                    for e in range(ET):
                        last = pe.transpose(ps[1][:, e * P:(e + 1) * P], xt[:, e, t * P:(t + 1) * P], ident[:])
                    last.then_inc(s["x1_ps"], 1)
                    if t > 0:
                        pe.wait_ge(s["x16_ok"], ET * bb + t)
                    for low, x16 in ((0, xh), (1, xl)):
                        for e in range(ET):
                            at = DI * low + e * P
                            last = pe.transpose(rows[:, at:at + P], x16[:, e, t * P:(t + 1) * P], ident16[:])
                    last.then_inc(s["x16_ps"], 1)

            def end_of_link(bb, ahead):
                if ahead:
                    x_projection(bb + 1)
                    dt_projection(bb + 1)
                router(bb)

            def up_part(g, slot, count, part):
                bank, used, ready = ((ps_g, "g_used", "g_ready"), (ps_u, "u_used", "u_ready"))[part]
                pe.wait_ge(up_in[slot], count)
                pe.wait_ge(s[used], g + 1)
                n = 0
                for k in range(ET):
                    for low, rhs in ((0, xh), (0, xl), (1, xh)):
                        at = UPW * low + 512 * part + P * k
                        last = pe.matmul(bank[:], wup[:, slot, at:at + P], rhs[:, k, :],
                                         start=(n == 0), stop=(n == 3 * ET - 1))
                        n += 1
                last.then_inc(s[ready], 1)

            def up(g, slot, count):
                up_part(g, slot, count, 0)
                up_part(g, slot, count, 1)

            def down(g, slot, count, closing=False):
                pe.wait_ge(down_in[slot], count)
                pe.wait_ge(s["hlo_done"], g + 1)
                for m in range(ET):
                    for n, (low, lhs) in enumerate(((0, hhi), (1, hhi), (0, hlo))):
                        last = pe.matmul(acc[:, m, :], lhs[:, slot, P * m:P * (m + 1)],
                                         wdown[:, slot, DNW * low:DNW * (low + 1)],
                                         start=False, stop=(closing and n == 2), skip_group_check=True)
                last.then_inc(s["down_done"], 1)

            def shared(b, beside, ahead=False):
                def up_of(c):
                    up(CH * b + c, c % 2, 16 * fills(b, c))

                def down_of(c):
                    down(CH * b + c, c % 2, 16 * fills(b, c), closing=(c == CH - 1))

                turn(b, range(ET))
                if beside:
                    pe.wait_ge(s["dtv_ok"], ET * (b + 2))
                pe.wait_ge(s["xl_ok"], ET * (b + 1))
                up_of(0)
                if not beside:
                    prefix()
                up_of(1)
                pe.wait_ge(s["fin_ok"], b + 1)
                for m in range(ET):
                    pe.matmul(acc[:, m, :], zeros16[:], xh[:, m, :], start=True, stop=False, skip_group_check=True)
                down_of(0)
                if beside:
                    pe.wait_ge(s["x1tok_ok"], ET * (b + 1))
                    pe.wait_ge(s["x16_ok"], ET * (b + 1))
                    for e in range(2):
                        pe.matmul(ps[e][:], zeros16[:], xh[:, 0, :], start=True, stop=False, skip_group_check=True)
                    for e in range(2):
                        y_add(SL * (b + 1) + e, prod_pe, e, ps[e][:])
                up_of(2)
                down_of(1)

                def double(tt):
                    for i in range(2):
                        g = CH * b + C0 + 2 * tt + i
                        count = 16 * (S_OF[1 - i] * b + tt + 2 + i)
                        gs = SL * (b + 1) + ET * (2 * tt + i)
                        summing = beside and not (isinstance(tt, int) and tt == 0 and i == 0)
                        up_part(g + 1, 1 - i, count, 0)
                        if summing:
                            y_add(gs, prod_pe, 0, ps[0][:])
                        up_part(g + 1, 1 - i, count, 1)
                        if summing:
                            y_add(gs + 1, prod_pe, 1, ps[1][:])
                        down(g, i, 16 * (S_OF[i] * b + tt + 2))

                double(0)
                with pe.Fori(1, NP // 2 - 1) as tt:
                    double(tt)
                if not beside:
                    pe.wait_ge(s["rows_ok"], 1)
                    pe.transpose(ps[1][:, 0:NT], rows_f[:], ident[0:NT, 0:NT]).then_inc(s["list_ps"], 1)
                double(NP // 2 - 1)
                down_of(CH - 1)
                if ahead:
                    in_projection(b + 2, False, (0, 1))
                if beside:
                    mean(b + 1)
                if ahead:
                    in_projection(b + 2, False, (2, 3))
                if beside:
                    variance(b + 1)
                    end_of_link(b + 1, ahead)

            def prefix():
                pe.wait_ge(s["x16_ok"], TT)
                pe.wait_ge(s["hot_ok"], 2)
                pe.matmul(ps[0][:, 0:E * TT], tri[:], count16[:], start=True, stop=True)
                pe.matmul(ps[0][:, E * TT:2 * E * TT], ones16[:], count16[:], start=True, stop=True)\
                    .then_inc(s["prefix_ok"], 1)

            def turn_x(i, slot, listed, first=False):
                pe.wait_ge(list_in[slot], 16 * listed)
                if not first:
                    pe.wait_ge(s["xt_ok"], i)
                rows = ps[0][:].bitcast(F16)
                for n in range(2 * ET):
                    last = pe.transpose(rows[:, n * P:(n + 1) * P], xst[:, slot, n * P:(n + 1) * P], ident16[:])
                last.then_inc(s["xt_ps"], 1)

            def expert_of(i):
                return pe.value_load(tid[0:1, bass.ds(i, 1)], min_val=0, max_val=E - 1)

            def expert_up(i, slot, e, part):
                bank = acc[:, 2 * slot + part, 0:I_MOE]
                n = 0
                for k in range(ET):
                    for xlow, wlow in ((0, 0), (0, 1), (1, 0)):
                        at = XUP * wlow + 2 * I_MOE * k + I_MOE * part
                        last = pe.matmul(bank, xgt[:, slot, (ET * xlow + k) * P:(ET * xlow + k + 1) * P],
                                         wall[:, bass.ds(e, 1), at:at + I_MOE].rearrange("p a b -> p (a b)"),
                                         start=(n == 0), stop=(n == 3 * ET - 1))
                        n += 1
                last.then_inc(s["eu_ready" if part else "eg_ready"], 1)

            def turn_h(i, slot, first=False):
                pe.wait_ge(s["elo_done"], i + 1)
                if not first:
                    pe.wait_ge(s["ht_ok"], i)
                rows = ps[1][:].bitcast(F16)
                for low, h16 in ((0, hhi), (1, hlo)):
                    for k in range(KH):
                        n = KH * low + k
                        last = pe.transpose(rows[:, n * P:(n + 1) * P], h16[:, slot, k * P:(k + 1) * P], ident16[:])
                last.then_inc(s["ht_ps"], 1)

            def expert_down(i, slot, e, settled=True):
                pe.wait_ge(s["ht_ok"], i + 1)
                if settled:
                    pe.wait_ge(s["y_ok"], i - 1)
                n = 0
                for k in range(KH):
                    for hlow, wlow in ((0, 0), (0, 1), (1, 0)):
                        at = 2 * XUP + XDN * wlow + DI * k
                        last = pe.matmul(ps_y[slot][:], ht[:, slot, (KH * hlow + k) * P:(KH * hlow + k + 1) * P],
                                         wall[:, bass.ds(e, 1), at:at + DI].rearrange("p a b -> p (a b)"),
                                         start=(n == 0), stop=(n == 3 * KH - 1))
                        n += 1
                last.then_inc(s["edown_done"], 1)

            def expert_step(i, slot, listed, opening=False, closing=False, settled=True):
                e = expert_of(i)
                if not closing:
                    turn_x(i + 1, 1 - slot, listed)
                pe.wait_ge(s["xt_ok"], i + 1)
                if settled:
                    pe.wait_ge(s["eh_done"], i - 1)
                expert_up(i, slot, e, 0)
                if not opening:
                    turn_h(i - 1, 1 - slot, not settled)
                expert_up(i, slot, e, 1)
                if not opening:
                    expert_down(i - 1, 1 - slot, expert_of(i - 1), not (isinstance(i, int) and i <= 2))

            pe.wait_ge(s["win_in"], 16)
            in_projection(0, True, range(ET))
            pe.wait_ge(s["consts"], NCONST)
            pe.wait_ge(s["const_dve"], 6)
            x_projection(0)
            dt_projection(0)
            for e in range(ET):
                y_add(e, prod, e % 2, y_bank0[e], start=True)
            with pe.Fori(1, NP) as t:
                for e in range(ET):
                    y_add(ET * t + e, prod, e % 2, y_bank0[e])
            in_projection(1, False, (0, 1))
            mean(0)
            in_projection(1, False, (2, 3))
            variance(0)
            end_of_link(0, True)
            with pe.Fori(0, B - 2) as b:
                shared(b, True, True)
            shared(B - 2, True)
            shared(B - 1, False)
            turn_x(0, 0, 1, first=True)
            pe.wait_ge(s["experts_lo"], PIECES)
            pe.wait_ge(s["fin_ok"], B + 1)
            pe.wait_ge(s["assigned"], ASSIGN)
            expert_step(0, 0, 1, opening=True, settled=False)
            expert_step(1, 1, 2, settled=False)
            expert_step(2, 0, 2)
            expert_step(3, 1, 3)
            with pe.Fori(2, (NT - 1) // 2) as t:
                expert_step(2 * t, 0, t + 1)
                expert_step(2 * t + 1, 1, t + 2)
            expert_step(NT - 1, 0, 0, closing=True)
            turn_h(NT - 1, 0)
            expert_down(NT - 1, 0, expert_of(NT - 1))

        @block.scalar
        def _(act):
            def row_rstd(bb):
                act.wait_ge(s["bn_aggr"], ET * (bb + 1))
                act.activation(lnv[:], mv[:, :, 1], ACT.Ln, bias=eps[:, 0:1]).then_inc(s["ln1"], 1)
                act.wait_ge(s["ln1"], bb + 1)
                act.activation(rstd[:], lnv[:], ACT.Exp, scale=-0.5).then_inc(s["rstd_ok"], 1)

            def projected(bb):
                act.wait_ge(s["pads"], bb + 1)
                for e in range(ET):
                    act.wait_ge(s["inproj"], ET * bb + e + 1)
                    act.activation(xp[:, e, DC - 1:DC - 1 + L], ps_y[e % 2][:], ACT.Copy).then_inc(s["xp_ok"], 1)

            def squash_conv(bb):
                for e in range(ET):
                    act.wait_ge(s["conv"], DC * (ET * bb + e + 1))
                    act.activation(tmp_c[:, e, :], delta[:, e, :], ACT.Tanh, scale=0.5).then_inc(s["tanh_u"], 1)

            def squash_z(bb):
                act.wait_ge(s["front_ok"], ET * (bb + 1))
                act.wait_ge(s["z_ok"], ET * (bb + 1))
                act.activation(tmp_a[:], xn[:], ACT.Tanh, scale=0.5).then_inc(s["tz_ok"], 1)

            def x_rows(bb):
                act.wait_ge(s["xproj_ok"], bb + 1)
                act.activation(xdbl[:], ps_y[0][0:XD, :], ACT.Copy, scale=0.5).then_inc(s["xdbl_ok"], 1)

            def skip(bb):
                for e in range(ET):
                    act.wait_ge(s["u_ok"], ET * bb + e + 1)
                    act.activation(y2[:, e, 0, :], du[:, e, :], ACT.Copy, scale=dhalf[:, e:e + 1]).then_inc(s["y_init"], 1)

            def dt_rows(bb):
                for e in range(ET):
                    act.wait_ge(s["dt_ok"], ET * bb + e + 1)
                    act.activation(tmp_a[:, e, :], ps_y[e % 2][:], ACT.Abs, bias=dtb[:, e:e + 1])
                    act.activation(vt[:, e, :], ps_y[e % 2][:], ACT.Identity, bias=dtb[:, e:e + 1])\
                        .then_inc(s["dtv_ok"], 1)

            def exp_rows(bb):
                for e in range(ET):
                    act.wait_ge(s["dtv_ok"], ET * bb + e + 1)
                    act.activation(tmp_a[:, e, :], tmp_a[:, e, :], ACT.Exp, scale=-1.0).then_inc(s["e1_ok"], 1)

            def log_rows(bb):
                for e in range(ET):
                    act.wait_ge(s["e1_ok"], ET * bb + e + 1)
                    act.activation(tmp_c[:, e, :], tmp_a[:, e, :], ACT.Ln, bias=one[:, 0:1]).then_inc(s["ln_ok"], 1)

            def decay(gs, t, e):
                act.wait_ge(s["scan_done"], gs + 1)
                act.activation(da[:, e % 2, 0, :], delta[:, e, :], ACT.Exp, scale=amat[:, e, bass.ds(2 * t, 1)])
                act.activation(da[:, e % 2, 1, 1:L], delta[:, e, 1:L], ACT.Exp, scale=amat[:, e, bass.ds(2 * t + 1, 1)])\
                    .then_inc(s["da_ready"], 1)

            def squares(bb):
                for e in range(ET):
                    act.wait_ge(s["xc_ok"], ET * bb + e + 1)
                    act.activation(tmp_c[:, e, :], tb[:, e, :], ACT.Square).then_inc(s["sq_ok"], 1)

            def token_rstd(bb):
                act.wait_ge(s["var_ok"], bb + 1)
                act.activation(tmp_a[:, 0, :], ps[1][:], ACT.Ln, bias=eps[:, 0:1]).then_inc(s["ln2"], 1)
                act.wait_ge(s["ln2"], bb + 1)
                act.activation(tmp_a[:, 1, :], tmp_a[:, 0, :], ACT.Exp, scale=-0.5).then_inc(s["rs_ok"], 1)

            def x_high(bb, first):
                if not first:
                    act.wait_ge(s["u_ready"], CH * bb)
                for e in range(ET):
                    act.wait_ge(s["xnorm"], ET * bb + e + 1)
                    act.activation(xh[:, e, :], tb[:, e, :], ACT.Copy).then_inc(s["xh_ok"], 1)

            def router_exps(bb):
                act.wait_ge(s["gap_ok"], bb + 1)
                act.activation(e2[:], gap[:], ACT.Exp).then_inc(s["e2_ok"], 1)
                act.activation(sg[:], lg[:, :, E], ACT.Tanh, scale=0.5).then_inc(s["tsg"], 1)

            def rows_out(bb, tiles):
                for t in tiles:
                    if t == 0:
                        act.wait_ge(s["fin_ok"], bb + 1)
                        act.wait_ge(s["base_out"], 16 * bb + 1)
                    act.wait_ge(s["x1_ps"], ET * bb + t + 1)
                    act.activation(x1tok[:, t, :], ps[1][:], ACT.Copy).then_inc(s["x1tok_ok"], 1)
                    if t == 0:
                        act.wait_ge(s["x16_stored"], 16 * bb + 1)
                    act.wait_ge(s["x16_ps"], ET * bb + t + 1)
                    act.activation(xst[:, t, :], ps[0][:].bitcast(F16), ACT.Copy).then_inc(s["x16_ok"], 1)

            def end_of_link(bb, ahead):
                if ahead:
                    x_rows(bb + 1)
                    dt_rows(bb + 1)
                    exp_rows(bb + 1)
                    log_rows(bb + 1)
                    row_rstd(bb + 1)
                router_exps(bb)

            def squash(g):
                act.wait_ge(s["g_ready"], g + 1)
                act.activation(th, ps_g[:], ACT.Tanh, scale=0.5 / WS).then_inc(s["tanh_done"], 1)

            def high(g, slot):
                act.wait_ge(s["u_used"], g + 2)
                act.activation(hhi[:, slot, :], hf, ACT.Copy).then_inc(s["hi_done"], 1)

            def split(i):
                act.activation(wup[:, i, 0:UPW], w32[:, i, 0:UPW], ACT.Copy, scale=WS)
                act.activation(wdown[:, i, 0:DNW], w32[:, i, UPW:HALF], ACT.Copy, scale=WS).then_inc(s["prep_hi"], 1)

            def split_early(c):
                act.wait_ge(raw_in[c % 2], 16 * (c // 2 + 1))
                if c >= 2:
                    act.wait_ge(stored[c % 2], 32 * (c // 2))
                split(c % 2)

            def split_piece(j):
                e, src, cols, at, step, raw = piece(j)
                arrived(act, j)
                if 0 < e <= EARLY:
                    act.wait_ge(s["experts_lo"], 3 * e)
                act.activation(wall[:, e, at:at + cols], raw, ACT.Copy, scale=WS).then_inc(s["experts_hi"], 1)

            def x_turned(i, slot):
                act.wait_ge(s["xt_ps"], i + 1)
                act.activation(xgt[:, slot, :], ps[0][:].bitcast(F16), ACT.Copy).then_inc(s["xt_ok"], 1)

            def expert_squash(i, slot):
                act.wait_ge(s["eg_ready"], i + 1)
                act.activation(th[:, 0:I_MOE], acc[:, 2 * slot, 0:I_MOE], ACT.Tanh, scale=0.5 / WS)\
                    .then_inc(s["etanh_done"], 1)

            def expert_high(i, slot):
                act.wait_ge(s["eh_done"], i + 1)
                act.activation(hhi[:, slot, 0:I_MOE], hf[:, 0:I_MOE], ACT.Copy).then_inc(s["ehi_done"], 1)

            def expert_out(i, slot, count=None):
                act.wait_ge(s["edown_done"], i + 1)
                if count is not None:
                    act.wait_ge(y_out[slot], 16 * count)
                act.activation(yout[:, slot, :], ps_y[slot][:], ACT.Copy).then_inc(s["y_ok"], 1)

            act.wait_ge(s["consts"], NCONST)
            act.activation(amat[:], amat[:], ACT.Exp).then_inc(s["const_act"], 1)
            act.activation(gates[:, 0:2], gates[:, 0:2], ACT.Tanh).then_inc(s["const_act"], 1)
            act.wait_ge(s["const_dve"], 4)
            act.wait_ge(s["const_dve2"], 3)
            projected(0)
            squash_conv(0)
            skip(0)
            split_early(0)
            x_rows(0)
            dt_rows(0)
            exp_rows(0)
            log_rows(0)
            row_rstd(0)

            def pairs0(tt):
                for i in range(2):
                    for e in range(ET):
                        if isinstance(tt, int) and i == 0:
                            act.wait_ge(s["front_ok"], e + 1)
                        decay(ET * (2 * tt + i) + e, 2 * tt + i, e)
                    act.wait_ge(raw_in[1 - i], 16 * (tt + 1 + i))
                    if not (isinstance(tt, int) and i == 0):
                        act.wait_ge(stored[1 - i], 32 * (tt + i))
                    split(1 - i)

            pairs0(0)
            squash_z(0)
            with act.Fori(1, NP // 2) as tt:
                pairs0(tt)
            for c in range(NP + 1, CH):
                split_early(c)
            projected(1)
            squares(0)
            token_rstd(0)
            x_high(0, True)
            squash_conv(1)
            skip(1)
            end_of_link(0, True)

            def shared(b, beside, ahead=False):
                def both(c):
                    squash(CH * b + c)
                    high(CH * b + c, c % 2)

                if beside:
                    def pairs(tt):
                        for i in range(2):
                            start = isinstance(tt, int) and i == 0
                            second = isinstance(tt, int) and i == 1
                            g = CH * b + C0 + 2 * tt + i
                            gs = SL * (b + 1) + ET * (2 * tt + i)
                            for e in range(ET):
                                if start:
                                    act.wait_ge(s["front_ok"], ET * (b + 1) + e + 1)
                                if start and e < 2:
                                    rows_out(b, (e,))
                                decay(gs + e, 2 * tt + i, e)
                                if e == 1 and start:
                                    rows_out(b, (2, 3))
                                if start and e == 2:
                                    both(0)
                                if start and e == 3:
                                    both(1)
                                if second and e == 1:
                                    both(2)
                                if not start and e == (2 if second else 1):
                                    squash(g)
                                if not start and e == (3 if second else 2):
                                    high(g, i)

                    pairs(0)
                    squash_z(b + 1)
                    with act.Fori(1, NP // 2) as tt:
                        pairs(tt)
                    both(CH - 1)
                    if ahead:
                        projected(b + 2)
                    squares(b + 1)
                    token_rstd(b + 1)
                    x_high(b + 1, False)
                    if ahead:
                        squash_conv(b + 2)
                        skip(b + 2)
                    end_of_link(b + 1, ahead)
                else:
                    rows_out(b, range(ET))
                    both(0)
                    both(1)
                    act.wait_ge(s["lg_ok"], B)
                    act.wait_ge(s["xl_ok"], ET * B)
                    for c in range(CH):
                        if c >= 2:
                            both(c)
                        for j in range(split_by[c] - beside_chunk[c], split_by[c]):
                            split_piece(j)

            with act.Fori(0, B - 2) as b:
                shared(b, True, True)
            shared(B - 2, True)
            shared(B - 1, False)
            x_turned(0, 0)
            x_turned(1, 1)
            expert_squash(0, 0)
            expert_high(0, 0)

            x_turned(2, 0)
            expert_squash(1, 1)
            expert_high(1, 1)
            expert_out(0, 0)

            x_turned(3, 1)
            expert_squash(2, 0)
            expert_high(2, 0)
            expert_out(1, 1)
            with act.Fori(1, (NT - 3) // 2) as t:
                for i in range(2):
                    n = 2 * t + 1 + i
                    x_turned(n + 1, i)
                    expert_squash(n, 1 - i)
                    expert_high(n, 1 - i)
                    expert_out(n - 1, i, t)
            n = NT - 2
            x_turned(n + 1, 0)
            expert_squash(n, 1)
            expert_high(n, 1)
            expert_out(n - 1, 0, (n - 1) // 2)
            expert_squash(n + 1, 0)
            expert_high(n + 1, 0)
            expert_out(n, 1, n // 2)
            expert_out(n + 1, 0, (n + 1) // 2)

        @block.vector
        def _(ve):
            def pads(bb, first):
                if not first:
                    ve.wait_ge(s["ysum"], ET * bb)
                ve.memset(xp[:, :, 0:DC - 1], 0.0).then_inc(s["pads"], 1)

            def row_stats(bb):
                ve.wait_ge(s["xn_in"], 16 * (bb + 1))
                for e in range(ET):
                    ve.bn_stats(stats[:, e, :], xn[:, e, :]).then_inc(s["bn_stats"], 1)
                ve.wait_ge(s["bn_stats"], ET * (bb + 1))
                ve.memset(carry[:], 0.0)
                for e in range(ET):
                    ve.bn_aggr(mv[:, e, :], stats[:, e, :]).then_inc(s["bn_aggr"], 1)

            def convolution(bb, tiles=range(ET)):
                n = DC * ET * bb
                for e in tiles:
                    ve.wait_ge(s["xp_ok"], ET * bb + e + 1)
                    ve.tensor_scalar(delta[:, e, :], xp[:, e, 0:L], cw[:, e, 0:1], cbias[:, e:e + 1], ALU.mult, ALU.add)\
                        .then_inc(s["conv"], 1)
                    for k in range(1, DC):
                        ve.wait_ge(s["conv"], n + DC * e + k)
                        ve.scalar_tensor_tensor(out=delta[:, e, :], in0=xp[:, e, k:k + L], scalar=cw[:, e, k:k + 1],
                                                in1=delta[:, e, :], op0=ALU.mult, op1=ALU.add).then_inc(s["conv"], 1)

            def normed_rows(bb):
                ve.wait_ge(s["rstd_ok"], bb + 1)
                for e in range(ET):
                    ve.tensor_scalar(xn[:, e, :], xn[:, e, :], mv[:, e, 0:1], rstd[:, e:e + 1], ALU.subtract, ALU.mult)\
                        .then_inc(s["z_ok"], 1)

            def silu_u(bb):
                for e in range(ET):
                    ve.wait_ge(s["tanh_u"], ET * bb + e + 1)
                    ve.scalar_tensor_tensor(out=du[:, e, :], in0=tmp_c[:, e, :], scalar=1.0, in1=delta[:, e, :],
                                            op0=ALU.add, op1=ALU.mult).then_inc(s["u_ok"], 1)

            def silu_z(bb):
                ve.wait_ge(s["tz_ok"], bb + 1)
                ve.scalar_tensor_tensor(out=xn[:], in0=tmp_a[:], scalar=1.0, in1=xn[:], op0=ALU.add, op1=ALU.mult)\
                    .then_inc(s["gate_ok"], 1)

            def softplus(bb):
                n = ET * bb
                for e in range(ET):
                    ve.wait_ge(s["e1_ok"], n + e + 1)
                    ve.scalar_tensor_tensor(out=delta[:, e, :], in0=vt[:, e, :], scalar=0.0, in1=tmp_a[:, e, :],
                                            op0=ALU.max, op1=ALU.add)
                    ve.tensor_scalar(st[:, e // 2, e % 2, :], tmp_a[:, e, :], 1.0, 1.0, ALU.add, ALU.subtract).then_inc(s["x_ok"], 1)
                for e in range(ET):
                    ve.wait_ge(s["x_ok"], n + e + 1)
                    ve.tensor_tensor(delta[:, e, :], delta[:, e, :], st[:, e // 2, e % 2, :], ALU.subtract).then_inc(s["corr_ok"], 1)

            def softplus_end(bb):
                n = ET * bb

                def whole(e):
                    ve.wait_ge(s["corr_ok"], n + e + 1)
                    ve.wait_ge(s["ln_ok"], n + e + 1)
                    ve.tensor_tensor(delta[:, e, :], delta[:, e, :], tmp_c[:, e, :], ALU.add).then_inc(s["delta_ok"], 1)

                def times_u(e):
                    ve.wait_ge(s["delta_ok"], n + e + 1)
                    if e == 0:
                        ve.wait_ge(s["y_init"], ET * (bb + 1))
                        ve.wait_ge(s["xproj_ok"], bb + 1)
                    ve.scalar_tensor_tensor(out=du[:, e, :], in0=delta[:, e, :], scalar=0.5, in1=du[:, e, :],
                                            op0=ALU.mult, op1=ALU.mult).then_inc(s["front_ok"], 1)

                whole(0)
                for e in range(1, ET):
                    whole(e)
                    times_u(e - 1)
                times_u(ET - 1)

            def scan(gs, e):
                ve.wait_ge(s["da_ready"], gs + 1)
                ve.wait_ge(s["dbu_ready"], gs + 1)
                ve.tensor_tensor_scan(st[:, e % 2, :, :].rearrange("p n l -> p (n l)"),
                                      da[:, e % 2, :, :].rearrange("p n l -> p (n l)"),
                                      dbu[:, e % 2, :, :].rearrange("p n l -> p (n l)"),
                                      0.0, ALU.mult, ALU.add).then_inc(s["scan_done"], 1)

            def readout(gs, slot, out_slot, slots=prod):
                ve.wait_ge(s["scan_done"], gs + SEED + 1)
                ve.tensor_tensor(slots[:, out_slot, :, :], st[:, out_slot, :, :], bc[:, slot, 2:4, :], ALU.mult)\
                    .then_inc(s["prod_ready"], 1)

            def split_low(c, i):
                ve.wait_ge(s["prep_hi"], c + 1)
                ve.scalar_tensor_tensor(out=wup[:, i, UPW:2 * UPW], in0=w32[:, i, 0:UPW], scalar=WS,
                                        in1=wup[:, i, 0:UPW], op0=ALU.mult, op1=ALU.subtract)
                ve.scalar_tensor_tensor(out=wdown[:, i, DNW:2 * DNW], in0=w32[:, i, UPW:HALF], scalar=WS,
                                        in1=wdown[:, i, 0:DNW], op0=ALU.mult, op1=ALU.subtract)\
                    .then_inc(s["prep_lo"], 1)

            def first_residual(bb, first):
                for h in range(0, ET, 2):
                    for e in (h, h + 1):
                        if first or e < 2:
                            part = y_bank0[e]
                            ve.wait_ge(s["y_pe"], SL + SEED - ET + e + 1 if first else SL + SEED + 2 * NP * bb - 1 + e)
                        else:
                            part = y2[:, e, 1, :]
                            ve.wait_ge(s["y_dve" if e == 2 else "y_pool"], NP * bb + 1)
                        if first and e == 0:
                            ve.wait_ge(s["gate_ok"], 1)
                        ve.tensor_tensor(tmp_a[:, e, :], y2[:, e, 0, :], part, ALU.add).then_inc(s["ysum"], 1)
                    for e in (h, h + 1):
                        ve.wait_ge(s["ysum"], ET * bb + e + 1)
                        ve.tensor_tensor(tmp_a[:, e, :], tmp_a[:, e, :], xn[:, e, :], ALU.mult).then_inc(s["yg"], 1)
                    for e in (h, h + 1):
                        ve.wait_ge(s["yg"], ET * bb + e + 1)
                        if e == 0:
                            ve.wait_ge(s["xt_in"], 16 * (bb + 1))
                        ve.scalar_tensor_tensor(out=xt[:, e, :], in0=tmp_a[:, e, :], scalar=gates[:, 0:1],
                                                in1=xt[:, e, :], op0=ALU.mult, op1=ALU.add).then_inc(s["x1_ok"], 1)

            def centre(bb):
                ve.wait_ge(s["mean_ok"], bb + 1)
                for e in range(ET):
                    ve.tensor_tensor(tb[:, e, :], xt[:, e, :], ps[0][:], ALU.subtract).then_inc(s["xc_ok"], 1)

            def normed(bb):
                ve.wait_ge(s["rs_ok"], bb + 1)
                ve.wait_ge(s["sq_ok"], ET * (bb + 1))
                for e in range(ET):
                    ve.tensor_tensor(tb[:, e, :], tb[:, e, :], tmp_a[:, 1, :], ALU.mult).then_inc(s["xnorm"], 1)

            def route(bb):
                ve.wait_ge(s["logits"], bb + 1)
                ve.tensor_copy(lg[:, :, 0:R], ps[0][:, 0:64].rearrange("p (t c) -> p t c", t=ET)[:, :, 0:R])\
                    .then_inc(s["lg_ok"], 1)
                ve.wait_ge(s["lg_ok"], bb + 1)
                ve.memset(carry[:], 0.0)
                for t in range(ET):
                    last = ve.max(top[:, t, :], lg[:, t, 0:E])
                last.then_inc(s["top_ok"], 1)
                ve.wait_ge(s["top_ok"], bb + 1)
                ve.tensor_tensor(gap[:], top[:, :, 1], top[:, :, 0], ALU.subtract).then_inc(s["gap_ok"], 1)
                for t in range(ET):
                    last = ve.max_index(topi[:, t, :], top[:, t, :], lg[:, t, 0:E])
                last.then_inc(s["topi_ok"], 1)
                ve.wait_ge(s["topi_ok"], bb + 1)
                ve.tensor_copy(choice[:, :, bass.ds(ET * bb, ET)].rearrange("p k t -> p t k"), topi[:, :, 0:2])
                ve.wait_ge(s["e2_ok"], bb + 1)
                ve.tensor_scalar(den[:], e2[:], 1.0, None, ALU.add).then_inc(s["den_ok"], 1)
                ve.wait_ge(s["den_ok"], bb + 1)
                ve.reciprocal(p1[:], den[:]).then_inc(s["p1_ok"], 1)
                ve.wait_ge(s["p1_ok"], bb + 1)
                ve.memset(carry[:], 0.0)
                ve.tensor_scalar(weight[:, 0, bass.ds(ET * bb, ET)], p1[:], gates[:, 1:2], None, ALU.mult)
                ve.scalar_tensor_tensor(out=weight[:, 1, bass.ds(ET * bb, ET)], in0=p1[:], scalar=gates[:, 1:2],
                                        in1=e2[:], op0=ALU.mult, op1=ALU.mult)
                ve.wait_ge(s["tsg"], bb + 1)
                ve.tensor_scalar(sgt[:], sg[:], 1.0, gates[:, 2:3], ALU.add, ALU.mult).then_inc(s["sgt_ok"], 1)

            def silu_gate(g):
                ve.wait_ge(s["tanh_done"], g + 1)
                ve.scalar_tensor_tensor(out=act_a, in0=th, scalar=1.0, in1=ps_g[:], op0=ALU.add, op1=ALU.mult)\
                    .then_inc(s["g_used"], 1)

            def hidden(g):
                ve.wait_ge(s["g_used"], g + 2)
                ve.wait_ge(s["u_ready"], g + 1)
                ve.scalar_tensor_tensor(out=hf, in0=act_a, scalar=HC, in1=ps_u[:], op0=ALU.mult, op1=ALU.mult)\
                    .then_inc(s["u_used"], 1)

            def low(g, slot):
                ve.wait_ge(s["hi_done"], g + 1)
                ve.tensor_tensor(hlo[:, slot, :], hf, hhi[:, slot, :], ALU.subtract).then_inc(s["hlo_done"], 1)

            def finish(b):
                ve.wait_ge(s["x1tok_ok"], ET * (b + 1))
                ve.wait_ge(s["sgt_ok"], b + 1)
                ve.wait_ge(s["down_done"], CH * (b + 1))
                for m in range(ET):
                    last = ve.scalar_tensor_tensor(out=x1tok[:, m, :], in0=acc[:, m, :], scalar=sgt[:, m:m + 1],
                                                   in1=x1tok[:, m, :], op0=ALU.mult, op1=ALU.add)
                last.then_inc(s["fin_ok"], 1)

            def one_hot():
                for e in range(E):
                    last = ve.tensor_scalar(hot[:, :, e, :], choice[:], float(e), None, ALU.is_equal)
                last.then_inc(s["hot_ok"], 1)
                ve.wait_ge(s["hot_ok"], 1)
                ve.tensor_tensor(count16[:].rearrange("p (e t) -> p e t", e=E), hot[:, 0], hot[:, 1], ALU.add)\
                    .then_inc(s["hot_ok"], 1)

            def assign():
                flat = "p e t -> p (e t)"
                done = s["assigned"]
                ve.wait_ge(s["prefix_ok"], 1)
                ve.tensor_copy(totals[:].rearrange(flat), ps[0][:, E * TT:2 * E * TT]).then_inc(done, 1)
                ve.wait_ge(done, 1)
                ve.tensor_tensor_scan(upto[:].rearrange(flat), keep[:].rearrange(flat), totals[:].rearrange(flat),
                                      0.0, ALU.mult, ALU.add).then_inc(done, 1)
                ve.wait_ge(done, 2)
                ve.tensor_tensor(more[:], upto[:, :, TT - 1:TT].broadcast_to([P, E, TT]), steps[:], ALU.is_gt)\
                    .then_inc(done, 1)
                ve.wait_ge(done, 3)
                ve.tensor_reduce(ntiles[:], more[:], AX.X, ALU.add).then_inc(done, 1)
                ve.wait_ge(done, 4)
                ve.tensor_tensor_scan(tend[:], keep[:, 0, 1:1 + E], ntiles[:], 0.0, ALU.mult, ALU.add).then_inc(done, 1)
                ve.wait_ge(done, 5)
                ve.tensor_tensor(first[:], tend[:], ntiles[:], ALU.subtract).then_inc(done, 1)
                ve.tensor_tensor(upto[:], upto[:], totals[:], ALU.subtract).then_inc(done, 1)
                ve.wait_ge(done, 7)
                ve.tensor_tensor(place[:].rearrange(flat), ps[0][:, 0:E * TT], upto[:].rearrange(flat), ALU.add)\
                    .then_inc(done, 1)
                ve.wait_ge(done, 8)
                ve.scalar_tensor_tensor(out=place[:], in0=first[:].rearrange("p (e o) -> p e o", o=1).broadcast_to([P, E, TT]),
                                        scalar=float(P), in1=place[:], op0=ALU.mult, op1=ALU.add).then_inc(done, 1)
                ve.wait_ge(done, 9)
                ve.tensor_tensor(hot[:, 0], hot[:, 0], place[:], ALU.mult)
                ve.tensor_tensor(hot[:, 1], hot[:, 1], place[:], ALU.mult).then_inc(done, 1)
                ve.wait_ge(done, 10)
                ve.tensor_reduce(posf[:], hot[:].rearrange("p k e t -> p k t e"), AX.X, ALU.add).then_inc(done, 1)
                ve.wait_ge(done, 11)
                ve.tensor_copy(pos[:], posf[:]).then_inc(done, 1)
                ve.tensor_tensor(past[:], index[:], tend[:].rearrange("p (o e) -> p o e", o=1).broadcast_to([P, NT, E]),
                                 ALU.is_ge).then_inc(done, 1)
                ve.wait_ge(done, 13)
                ve.tensor_reduce(tidf[:], past[:], AX.X, ALU.add).then_inc(done, 1)
                ve.wait_ge(done, 14)
                ve.tensor_scalar(tid[:], tidf[:], float(E - 1), None, ALU.min).then_inc(done, 1)

            def low_piece(j):
                e, src, cols, at, step, raw = piece(j)
                ve.wait_ge(s["experts_hi"], j + 1)
                ve.scalar_tensor_tensor(out=wall[:, e, at + step:at + step + cols], in0=raw, scalar=WS,
                                        in1=wall[:, e, at:at + cols], op0=ALU.mult, op1=ALU.subtract)\
                    .then_inc(s["experts_lo"], 1)

            def expert_silu(i, slot):
                ve.wait_ge(s["etanh_done"], i + 1)
                ve.scalar_tensor_tensor(out=act_a[:, 0:I_MOE], in0=th[:, 0:I_MOE], scalar=1.0,
                                        in1=acc[:, 2 * slot, 0:I_MOE], op0=ALU.add, op1=ALU.mult)\
                    .then_inc(s["egs_done"], 1)

            def expert_hidden(i, slot):
                ve.wait_ge(s["egs_done"], i + 1)
                ve.wait_ge(s["eu_ready"], i + 1)
                ve.scalar_tensor_tensor(out=hf[:, 0:I_MOE], in0=act_a[:, 0:I_MOE], scalar=HC,
                                        in1=acc[:, 2 * slot + 1, 0:I_MOE], op0=ALU.mult, op1=ALU.mult)\
                    .then_inc(s["eh_done"], 1)
                ve.wait_ge(s["ehi_done"], i + 1)
                ve.tensor_tensor(hlo[:, slot, 0:I_MOE], hf[:, 0:I_MOE], hhi[:, slot, 0:I_MOE], ALU.subtract)\
                    .then_inc(s["elo_done"], 1)

            def h_turned(i, slot):
                ve.wait_ge(s["ht_ps"], i + 1)
                ve.tensor_copy(ht[:, slot, :], ps[1][:].bitcast(F16)[:, 0:2 * HP]).then_inc(s["ht_ok"], 1)

            def expert_step(i, slot):
                h_turned(i - 1, 1 - slot)
                expert_silu(i, slot)
                expert_hidden(i, slot)

            ve.memset(mean_w[:], 1.0 / DI).then_inc(s["const_dve"], 1)
            ve.memset(zeros16[:], 0.0).then_inc(s["const_dve"], 1)
            ve.memset(eps[:], EPS).then_inc(s["const_dve"], 1)
            ve.memset(one[:], 1.0).then_inc(s["const_dve"], 1)
            ve.memset(ones16[:], 1.0).then_inc(s["const_dve"], 1)
            ve.memset(listed[:], 0).then_inc(s["const_dve"], 1)
            ve.memset(keep[:, :, 0:1], 0.0)
            ve.memset(keep[:, :, 1:TT], 1.0)
            for n in range(2):
                ve.memset(da[:, n, 1, 0:1], 0.0)
            at = 0
            for name, count in (("scan_done", SEED), ("y_pe", SEED), ("y_dve", 1), ("y_pool", 1), ("base_out", 1), ("x16_stored", 1), ("g_used", 1), ("u_used", 1), ("fin_ok", 1)):
                for n in range(count):
                    ve.memset(seedbox[:, at:at + 1], 0.0).then_inc(s[name], 1)
                    at += 1
            ve.wait_ge(s["consts"], NCONST)
            ve.wait_ge(s["const_act"], 2)
            ve.tensor_scalar(amat[:], amat[:], -1.0, None, ALU.mult).then_inc(s["const_dve2"], 1)
            ve.tensor_scalar(dhalf[:], dhalf[:], 0.5, None, ALU.mult).then_inc(s["const_dve2"], 1)
            ve.tensor_scalar(gates[:, 0:1], gates[:, 0:1], 0.5, None, ALU.mult)
            ve.tensor_scalar(gates[:, 1:2], gates[:, 1:2], 1.0 / (WS * HS), None, ALU.mult).then_inc(s["const_dve2"], 1)
            ve.wait_ge(s["const_dve2"], 3)
            ve.tensor_scalar(gates[:, 2:3], gates[:, 1:2], 0.5, None, ALU.mult).then_inc(s["const_dve2"], 1)
            ve.wait_ge(s["const_dve2"], 4)
            pads(0, True)
            convolution(0)
            silu_u(0)
            split_low(0, 0)
            row_stats(0)
            softplus(0)
            softplus_end(0)

            def pairs0(tt):
                for i in range(2):
                    t = 2 * tt + i
                    ve.wait_ge(bc_in[i], 16 * (tt + 1))
                    for e in range(ET):
                        scan(ET * t + e, e)
                        if e == 2:
                            split_low(t + 1, 1 - i)
                        ve.wait_ge(s["y_pe"], ET * t + e + 1)
                        readout(ET * t + e, i, e % 2)

            pairs0(0)
            normed_rows(0)
            with ve.Fori(1, NP // 2) as tt:
                pairs0(tt)
            silu_z(0)
            first_residual(0, True)
            pads(1, False)
            convolution(1, (0,))
            centre(0)
            convolution(1, (1, 2, 3))
            normed(0)
            silu_u(1)

            def end_of_link(bb, ahead):
                if ahead:
                    row_stats(bb + 1)
                    ve.memset(y2[:, 2:4, 1, :], 0.0).then_inc(s["y_zero"], 1)
                    if isinstance(bb, int) and bb == 0:
                        for c in range(NP + 1, CH):
                            split_low(c, c % 2)
                    softplus(bb + 1)
                route(bb)
                if ahead:
                    softplus_end(bb + 1)

            end_of_link(0, True)

            def shared(b, beside, ahead=False):
                def chunk(c):
                    silu_gate(CH * b + c)
                    hidden(CH * b + c)
                    low(CH * b + c, c % 2)

                if beside:
                    def pairs(tt):
                        for i in range(2):
                            t = 2 * tt + i
                            g = CH * b + C0 + t
                            gs = SL * (b + 1) + ET * t
                            start = isinstance(tt, int) and tt == 0 and i == 0
                            second = isinstance(tt, int) and tt == 0 and i == 1
                            ve.wait_ge(bc_in[i], 16 * (NP // 2 * (b + 1) + tt + 1))
                            scan(gs, 0)
                            ve.wait_ge(s["y_pe"], SL + SEED + 2 * NP * b + 2 * t - 1)
                            readout(gs, i, 0, prod_pe)
                            scan(gs + 1, 1)
                            if not start and not second:
                                silu_gate(g)
                            ve.wait_ge(s["y_pe"], SL + SEED + 2 * NP * b + 2 * t)
                            readout(gs + 1, i, 1, prod_pe)
                            if second:
                                chunk(2)
                            elif not start:
                                hidden(g)
                            scan(gs + 2, 2)
                            readout(gs + 2, i, 0)
                            if start:
                                chunk(0)
                            else:
                                if second:
                                    silu_gate(g)
                                    hidden(g)
                                low(g, i)
                            scan(gs + 3, 3)
                            ve.wait_ge(s["prod_ready"], gs + 3)
                            ve.wait_ge(s["y_dve"], NP * b + t + 1)
                            ve.tensor_tensor(y2[:, 2, :, :], y2[:, 2, :, :], prod[:, 0, :, :], ALU.add)\
                                .then_inc(s["y_dve"], 1)
                            ve.wait_ge(s["y_pool"], NP * b + t + 1)
                            readout(gs + 3, i, 1)
                            if start:
                                chunk(1)

                    ve.wait_ge(s["y_zero"], b + 1)
                    pairs(0)
                    normed_rows(b + 1)
                    with ve.Fori(1, NP // 2 - 1) as tt:
                        pairs(tt)
                    silu_z(b + 1)
                    pairs(NP // 2 - 1)
                    chunk(CH - 1)
                    first_residual(b + 1, False)
                    if ahead:
                        pads(b + 2, False)
                        convolution(b + 2, (0,))
                    centre(b + 1)
                    if ahead:
                        convolution(b + 2, (1, 2, 3))
                    normed(b + 1)
                    finish(b)
                    if ahead:
                        silu_u(b + 2)
                    end_of_link(b + 1, ahead)
                else:
                    one_hot()
                    chunk(0)
                    assign()
                    chunk(1)
                    for c in range(CH):
                        if c >= 2:
                            chunk(c)
                        if c == NP - 1:
                            ve.wait_ge(s["listed_in"], 16)
                            ve.tensor_copy(rows_f[:], rows_i[:]).then_inc(s["rows_ok"], 1)
                        if c == NP:
                            ve.wait_ge(s["list_ps"], 1)
                            ve.tensor_copy(listed[:], ps[1][:, 0:NT]).then_inc(s["listed_ok"], 1)
                        for j in range(split_by[c] - beside_chunk[c], split_by[c]):
                            low_piece(j)
                    finish(b)

            with ve.Fori(0, B - 2) as b:
                shared(b, True, True)
            shared(B - 2, True)
            shared(B - 1, False)
            ve.memset(hhi[:, :, I_MOE:HP], 0.0)
            ve.memset(hlo[:, :, I_MOE:HP], 0.0)
            expert_silu(0, 0)
            expert_hidden(0, 0)
            with ve.Fori(0, (NT - 1) // 2) as t:
                expert_step(2 * t + 1, 1)
                expert_step(2 * t + 2, 0)
            h_turned(NT - 1, 0)
            for h in range(TT // 2):
                pair = last_order[2 * h:2 * h + 2]
                ve.wait_ge(s["base_in"], 16 * (TT - ET - 2))
                if 0 in pair:
                    ve.wait_ge(s["late_in"], 32)
                ve.wait_ge(gathered[h], 64)
                for k in range(2):
                    if k == 1:
                        ve.wait_ge(s["first_sum"], h + 1)
                    for t in pair:
                        last = ve.scalar_tensor_tensor(out=base_tile(t), in0=y_of[k][:, t, :],
                                                       scalar=weight[:, k, t:t + 1], in1=base_tile(t),
                                                       op0=ALU.mult, op1=ALU.add)
                    last.then_inc(s["summed" if k else "first_sum"], 1)

        @block.gpsimd
        def _(pool):
            def inject(gs, slot, e):
                pool.wait_ge(s["scan_done"], gs + 1)
                pool.tensor_tensor(dbu[:, e % 2, :, :], du[:, e:e + 1, :].broadcast_to([P, 2, L]),
                                   bc[:, slot, 0:2, :], ALU.mult).then_inc(s["dbu_ready"], 1)

            def pair(bb, tt, slot, summing, opening=False):
                pool.wait_ge(bc_in[slot], 16 * (NP // 2 * bb + tt + 1))
                gs = SL * bb + ET * (2 * tt + slot)
                for e in range(ET):
                    if opening:
                        pool.wait_ge(s["front_ok"], ET * bb + e + 1)
                    inject(gs + e, slot, e)
                    if e == 1 and summing and not opening:
                        add(gs)

            def add(gs):
                pool.wait_ge(s["prod_ready"], gs)
                pool.tensor_tensor(y2[:, 3, :, :], y2[:, 3, :, :], prod[:, 1, :, :], ALU.add).then_inc(s["y_pool"], 1)

            def scan(bb, summing):
                if summing:
                    pool.wait_ge(s["y_zero"], bb)
                    pool.wait_ge(s["y_init"], ET * (bb + 1))
                pair(bb, 0, 0, summing, opening=True)
                pair(bb, 0, 1, summing)
                with pool.Fori(1, NP // 2) as tt:
                    pair(bb, tt, 0, summing)
                    pair(bb, tt, 1, summing)
                if summing:
                    add(SL * (bb + 1))

            def x_low(bb):
                for e in range(ET):
                    pool.wait_ge(s["xh_ok"], ET * bb + e + 1)
                    pool.tensor_tensor(xl[:, e, :], tb[:, e, :], xh[:, e, :], ALU.subtract).then_inc(s["xl_ok"], 1)

            scan(0, False)
            x_low(0)
            with pool.Fori(1, B) as bb:
                scan(bb, True)
                x_low(bb)

            pool.wait_ge(s["zeroed"], 16)
            pool.wait_ge(s["assigned"], 12)
            rows = bass.IndirectOffsetOnAxis
            for t in range(TT):
                for k in range(2):
                    pool.indirect_dma_start(list_dram, rows(ap=pos[:, k, t:t + 1], axis=0), token[:, t:t + 1], None)\
                        .then_inc(s["scattered"], 16)
            pool.wait_ge(s["scattered"], 16 * 2 * TT)
            pool.dma_start(rows_i[:], list_dram.rearrange("(t p) o -> t (p o)", p=P)).then_inc(s["listed_in"], 16)
            pool.wait_ge(s["listed_ok"], 1)
            pool.wait_ge(s["x16_stored"], 16 * B + 1)
            for i in range(NT):
                if i >= 2:
                    pool.wait_ge(s["xt_ps"], i - 1)
                pool.indirect_dma_start(xst[:, i % 2, :], None, x16_dram, rows(ap=listed[:, i:i + 1], axis=0))\
                    .then_inc(list_in[i % 2], 16)
            pool.wait_ge(y_out[0], 16 * ((NT + 1) // 2))
            pool.wait_ge(y_out[1], 16 * (NT // 2))
            for n, t in enumerate(last_order):
                for k in range(2):
                    pool.indirect_dma_start(y_of[k][:, t, :], None, y_dram, rows(ap=pos[:, k, t:t + 1], axis=0))\
                        .then_inc(gathered[n // 2], 16)


def kernel(x, ctx_1024, g_xattn, g_ffn, L0_xattn_in_proj_w, L0_xattn_conv_w, L0_xattn_conv_b, L0_xattn_x_proj_w,
           L0_xattn_dt_proj_w, L0_xattn_dt_proj_b, L0_xattn_A_log, L0_xattn_D, L0_ffn_router_weight,
           L0_ffn_gate_up_proj, L0_ffn_down_proj, L0_ffn_sh_gate_w, L0_ffn_sh_up_w, L0_ffn_sh_down_w,
           L0_ffn_shared_gate_w):
    import concourse.bacc as bacc
    from concourse.bass_utils import run_bass_kernel_spmd

    def tiles(a):
        return np.asarray(a).reshape(-1, P, a.shape[-1]).transpose(1, 0, 2)

    x = np.asarray(x)
    gu = np.asarray(L0_ffn_gate_up_proj)
    down = np.asarray(L0_ffn_down_proj).transpose(0, 2, 1)
    padded = np.zeros((E, HP, DI), np.float32)
    padded[:, :I_MOE] = down
    x_up = gu.transpose(0, 2, 1).reshape(E, 2, ET // 2, P, 2 * I_MOE).transpose(0, 1, 3, 2, 4)

    def by_chunk(w):
        return w.reshape(CH, P, ET, P).transpose(0, 3, 2, 1).reshape(CH, P, ET * P)

    arrays = {
        "x_nat": x.reshape(B, ET, P, L).transpose(0, 2, 1, 3),
        "x_t": x.transpose(0, 2, 1).reshape(B, ET, P, L).transpose(0, 2, 1, 3),
        "ctx_t": np.asarray(ctx_1024).transpose(0, 2, 1).reshape(B, KT, P, L).transpose(0, 2, 1, 3),
        "g_xattn": g_xattn,
        "g_ffn": g_ffn,
        "win_t": tiles(np.asarray(L0_xattn_in_proj_w).T),
        "conv_w": tiles(L0_xattn_conv_w),
        "conv_b": np.asarray(L0_xattn_conv_b).reshape(ET, P).T,
        "xproj_t": tiles(np.asarray(L0_xattn_x_proj_w).T),
        "dt_t": np.asarray(L0_xattn_dt_proj_w).T,
        "dt_b": np.asarray(L0_xattn_dt_proj_b).reshape(ET, P).T,
        "a_log": tiles(L0_xattn_A_log),
        "d_skip": np.asarray(L0_xattn_D).reshape(ET, P).T,
        "router_t": tiles(np.concatenate([L0_ffn_router_weight, L0_ffn_shared_gate_w]).T),
        "w_raw": np.concatenate([by_chunk(np.asarray(L0_ffn_sh_gate_w)), by_chunk(np.asarray(L0_ffn_sh_up_w)),
                                 np.asarray(L0_ffn_sh_down_w).T.reshape(CH, P, DI)], axis=2),
        "x_up": x_up.reshape(2 * E, P, ET * I_MOE),
        "x_down": padded.reshape(E, KH, P, DI).transpose(0, 2, 1, 3).reshape(E, P, KH * DI),
        "ident_in": np.eye(P, dtype=np.float32),
        "ident16_in": np.eye(P, dtype=np.float16),
        "tri_in": np.triu(np.ones((P, P), np.float16), 1),
        "steps_in": np.tile(P * np.arange(TT, dtype=np.float32), (P, E, 1)),
        "index_in": np.tile(np.arange(NT, dtype=np.float32)[:, None], (P, 1, E)),
        "token_in": np.arange(TT * P, dtype=np.int32).reshape(TT, P).T,
    }
    arrays = {k: np.ascontiguousarray(v) for k, v in arrays.items()}
    nc = bacc.Bacc("TRN2", target_bir_lowering=False, num_devices=1)
    aps = [nc.dram_tensor(k, v.shape, mybir.dt.from_np(v.dtype), kind="ExternalInput").ap() for k, v in arrays.items()]
    out = nc.dram_tensor("out_rows", (B, L, DI), F32, kind="ExternalOutput").ap()
    program(nc, *aps, out)
    r = run_bass_kernel_spmd(nc, [arrays], core_ids=[0])
    return r.results[0]["out_rows"]
```
